# Optimizing a Trainium2 kernel written in Bass

```python
import numpy as np
import jax
import jax.numpy as jnp

def _softmax(x, axis=-1):
    return jax.nn.softmax(x, axis=axis)

def _gelu(x):
    return jax.nn.gelu(x, approximate=True)

def _silu(x):
    return jax.nn.silu(x)

def _sigmoid(x):
    return jax.nn.sigmoid(x)

def _layernorm(x, axis=-1, eps=1e-05):
    m = jnp.mean(x, axis=axis, keepdims=True)
    v = jnp.var(x, axis=axis, keepdims=True)
    return (x - m) / jnp.sqrt(v + eps)

def _scatter_add(tgt, idx, src, axis=0):
    return tgt.at[idx].add(src)

def _segment_sum(src, seg, n):
    return jax.ops.segment_sum(src, seg, n)
kernel_name = 'mk_cond_resid_d2_seqx_r8_3fe478'

def setup_inputs(seed: int=0):
    np.random.seed(seed)
    _w = jnp.asarray

    def _rec_inputs():
        import jax
        import jax.numpy as jnp
        _rk = jax.random.key(seed)
        x = -7.109e-05 + 0.9999 * jax.random.normal(jax.random.fold_in(_rk, 1), (8, 128, 128), jnp.float32)
        _lenS = 128 - jax.random.randint(jax.random.fold_in(_rk, 7), (8,), 0, max(1, 128 // 4) + 1, jnp.int32)
        _lenS2 = 128 - jax.random.randint(jax.random.fold_in(_rk, 8), (8,), 0, max(1, 128 // 4) + 1, jnp.int32)
        itok_B_0_8 = jax.random.randint(jax.random.fold_in(_rk, 11), (8,), 0, 9, jnp.int32)
        itok_B_0_2 = jax.random.randint(jax.random.fold_in(_rk, 12), (8,), 0, 3, jnp.int32)
        return (x, itok_B_0_8, itok_B_0_2)
    x, itok_B_0_8, itok_B_0_2 = _rec_inputs()

    def _L0_cond_setup():
        import jax, jax.numpy as jnp
        import numpy as np
        LN_EPS = 1e-05
        key = jax.random.key(seed)
        ks = jax.random.split(key, 8)
        B, S, H, A, L = (32, 256, 128, 32, 10)
        return {'hidden_states': jax.random.normal(ks[0], (B, S, H), dtype=jnp.float32), 'language_ids': jax.random.randint(ks[1], (B,), 0, L, dtype=jnp.int64), 'W1': jax.random.normal(ks[2], (L, H, A), dtype=jnp.float32) * (1.0 / np.sqrt(H)), 'b1': jnp.zeros((L, A), dtype=jnp.float32), 'W2': jax.random.normal(ks[3], (L, A, H), dtype=jnp.float32) * (1.0 / np.sqrt(A)), 'b2': jnp.zeros((L, H), dtype=jnp.float32), 'gamma': jnp.ones((L, H), dtype=jnp.float32), 'beta': jnp.zeros((L, H), dtype=jnp.float32)}
    _L0_cond_all = _L0_cond_setup()
    _L0_cond_in = {k: v for k, v in _L0_cond_all.items() if k in ('W1', 'b1', 'W2', 'b2', 'gamma', 'beta')}
    del _L0_cond_all

    def _L1_cond_setup():
        import jax, jax.numpy as jnp
        import numpy as np
        B, S, D, F, E = (8, 128, 128, 512, 4)

        def _dense(x, wi, wo):
            return jax.nn.relu(x @ wi) @ wo
        key = jax.random.key(seed)
        ks = jax.random.split(key, 10)
        scale = 0.02
        return {'hidden_states': jax.random.normal(ks[0], (B, S, D), jnp.float32), 'type_idx': jax.random.randint(ks[1], (B,), 0, 3, jnp.int32), 'expert_wi': jax.random.normal(ks[2], (E, D, F), jnp.float32) * scale, 'expert_wo': jax.random.normal(ks[3], (E, F, D), jnp.float32) * scale, 'share_wi': jax.random.normal(ks[4], (3, D, F), jnp.float32) * scale, 'share_wo': jax.random.normal(ks[5], (3, F, D), jnp.float32) * scale, 'gate_vecs': jnp.array([[0.22, 0.22, 0.2, 0.2], [0.2, 0.22, 0.22, 0.2], [0.2, 0.2, 0.22, 0.22]], jnp.float32), 'gate_w1': jax.random.normal(ks[6], (4 * D, D), jnp.float32) * scale, 'gate_w2': jax.random.normal(ks[7], (D, 4), jnp.float32) * scale}
    _L1_cond_all = _L1_cond_setup()
    _L1_cond_in = {k: v for k, v in _L1_cond_all.items() if k in ('expert_wi', 'expert_wo', 'share_wi', 'share_wo', 'gate_vecs', 'gate_w1', 'gate_w2')}
    del _L1_cond_all
    return {'x': x, 'itok_B_0_8': itok_B_0_8, 'itok_B_0_2': itok_B_0_2, 'L0_cond_W1': _L0_cond_in['W1'], 'L0_cond_b1': _L0_cond_in['b1'], 'L0_cond_W2': _L0_cond_in['W2'], 'L0_cond_b2': _L0_cond_in['b2'], 'L0_cond_gamma': _L0_cond_in['gamma'], 'L0_cond_beta': _L0_cond_in['beta'], 'L1_cond_expert_wi': _L1_cond_in['expert_wi'], 'L1_cond_expert_wo': _L1_cond_in['expert_wo'], 'L1_cond_share_wi': _L1_cond_in['share_wi'], 'L1_cond_share_wo': _L1_cond_in['share_wo'], 'L1_cond_gate_vecs': _L1_cond_in['gate_vecs'], 'L1_cond_gate_w1': _L1_cond_in['gate_w1'], 'L1_cond_gate_w2': _L1_cond_in['gate_w2']}

def reference(x, itok_B_0_8, itok_B_0_2, L0_cond_W1, L0_cond_b1, L0_cond_W2, L0_cond_b2, L0_cond_gamma, L0_cond_beta, L1_cond_expert_wi, L1_cond_expert_wo, L1_cond_share_wi, L1_cond_share_wo, L1_cond_gate_vecs, L1_cond_gate_w1, L1_cond_gate_w2):
    import jax
    import jax.numpy as jnp

    def _L0_cond_ref(hidden_states, language_ids, W1, b1, W2, b2, gamma, beta):
        import jax, jax.numpy as jnp
        import numpy as np
        LN_EPS = 1e-05
        w1 = W1[language_ids]
        w2 = W2[language_ids]
        h = jnp.einsum('bsh,bha->bsa', hidden_states, w1) + b1[language_ids][:, None, :]
        h = jax.nn.relu(h)
        adapted = jnp.einsum('bsa,bah->bsh', h, w2) + b2[language_ids][:, None, :]
        x = hidden_states + adapted
        mean = jnp.mean(x, axis=-1, keepdims=True)
        var = jnp.mean(jnp.square(x - mean), axis=-1, keepdims=True)
        normed = (x - mean) * jax.lax.rsqrt(var + LN_EPS)
        return normed * gamma[language_ids][:, None, :] + beta[language_ids][:, None, :]

    def _L1_cond_ref(hidden_states, type_idx, expert_wi, expert_wo, share_wi, share_wo, gate_vecs, gate_w1, gate_w2):
        import jax, jax.numpy as jnp
        import numpy as np
        B, S, D, F, E = (8, 128, 128, 512, 4)

        def _dense(x, wi, wo):
            return jax.nn.relu(x @ wi) @ wo
        s0 = _dense(hidden_states, share_wi[0], share_wo[0])
        s1 = _dense(hidden_states, share_wi[1], share_wo[1])
        s2 = _dense(hidden_states, share_wi[2], share_wo[2])
        idx_a = type_idx
        idx_b = type_idx + 1
        out_a = jnp.einsum('bsf,bfd->bsd', jax.nn.relu(jnp.einsum('bsd,bdf->bsf', hidden_states, expert_wi[idx_a])), expert_wo[idx_a])
        out_b = jnp.einsum('bsf,bfd->bsd', jax.nn.relu(jnp.einsum('bsd,bdf->bsf', hidden_states, expert_wi[idx_b])), expert_wo[idx_b])
        p = jax.nn.softmax(gate_vecs / 0.1, axis=-1)
        wa = p[type_idx, idx_a][:, None, None]
        wb = p[type_idx, idx_b][:, None, None]
        expert_out = out_a * wa + out_b * wb
        gi = jnp.concatenate([expert_out[:, 0], s0[:, 0], s1[:, 0], s2[:, 0]], axis=-1)
        g = jax.nn.softmax(jax.nn.relu(gi @ gate_w1) @ gate_w2, axis=-1)
        out = expert_out * g[:, 0, None, None] + s0 * g[:, 1, None, None] + s1 * g[:, 2, None, None] + s2 * g[:, 3, None, None]
        return out
    x = x + _L0_cond_ref(x, itok_B_0_8, L0_cond_W1, L0_cond_b1, L0_cond_W2, L0_cond_b2, L0_cond_gamma, L0_cond_beta)
    x = x + _L1_cond_ref(x, itok_B_0_2, L1_cond_expert_wi, L1_cond_expert_wo, L1_cond_share_wi, L1_cond_share_wo, L1_cond_gate_vecs, L1_cond_gate_w1, L1_cond_gate_w2)
    return x

_drawn_inputs = setup_inputs


def setup_inputs(seed=0):
    import zlib

    import numpy as np

    out = dict(_drawn_inputs(seed))
    spreads = {'L0_cond_b1': (0.0, 0.1),
     'L0_cond_b2': (0.0, 0.1),
     'L0_cond_gamma': (1.0, 0.2),
     'L0_cond_beta': (0.0, 0.1)}
    factors = {'L1_cond_expert_wi': 8.0,
     'L1_cond_expert_wo': 8.0,
     'L1_cond_gate_vecs': 8.0,
     'L1_cond_gate_w1': 8.0,
     'L1_cond_gate_w2': 8.0}
    for name, (base, spread) in spreads.items():
        noise = np.random.default_rng([zlib.crc32(name.encode()), seed]).standard_normal(out[name].shape)
        drawn = base * np.exp(spread * noise) if base else spread * noise
        out[name] = jnp.asarray(drawn.astype(out[name].dtype))
    for name, factor in factors.items():
        out[name] = (out[name] * factor).astype(out[name].dtype)
    return out
```

```python
from contextlib import ExitStack

import concourse.bass as bass
from concourse import mybir



def conditional_residual_mlps(
    nc: bass.Bass,
    x: bass.AP,
    language: bass.AP,
    kind: bass.AP,
    W1: bass.AP,
    b1: bass.AP,
    W2: bass.AP,
    b2: bass.AP,
    gamma: bass.AP,
    beta: bass.AP,
    expert_wi: bass.AP,
    expert_wo: bass.AP,
    share_wi: bass.AP,
    share_wo: bass.AP,
    gate_vecs: bass.AP,
    gate_w1: bass.AP,
    gate_w2: bass.AP,
    out: bass.AP,
):
    f32 = mybir.dt.float32
    f32r = mybir.dt.float32r
    i32 = mybir.dt.int32
    ALU = mybir.AluOpType
    ACT = mybir.ActivationFunctionType
    AX = mybir.AxisListType

    B, S, D = x.shape
    L, _, A = W1.shape
    E, _, F = expert_wi.shape
    SH = share_wi.shape[0]
    T = gate_vecs.shape[0]
    P = 128
    HB = P // A
    NH = B // HB
    HT = HB * S
    FC = F // P
    M = SH + E
    UNITS = NH * SH * FC
    EPS = 1e-5
    assert S == P and D == P and HT == 512 and E == T + 1

    ctx = ExitStack()
    with ctx:
        def sb(name, shape, dt=f32):
            return ctx.enter_context(nc.sbuf_tensor(name, shape, dt))

        def sem(name):
            return ctx.enter_context(nc.semaphore(name))

        x_in = sb("x_in", [P, B, D])
        lang_row = sb("lang_row", [1, B], i32)
        lang_l = sb("lang_l", [L, B], i32)
        kind_row = sb("kind_row", [1, B], i32)
        kind_p = sb("kind_p", [P, B], i32)
        W1s = sb("W1s", [P, B, A])
        W2s = sb("W2s", [P, NH, D])
        b1_l = sb("b1_l", [L, HB, A])
        par_l = sb("par_l", [L, 3, D])
        gv = sb("gv", [P, T, E])
        gw1 = sb("gw1", [P, SH + 1, D])
        gw2 = sb("gw2", [P, SH + 1])
        w_raw = sb("w_raw", [P, 2, M, F])
        ident = sb("ident", [P, P])
        lang_no = sb("lang_no", [L, 1])
        lang_f = sb("lang_f", [L, B])
        onehot = sb("onehot", [L, B])
        b1_c = sb("b1_c", [P, B])
        par = sb("par", [P, B, 3, D])
        xT = sb("xT", [P, B * S])
        hbd = sb("hbd", [P, NH, HT])
        x_b2 = sb("x_b2", [P, B, D])
        x_beta = sb("x_beta", [P, B, D])
        y = sb("y", [P, B, D])
        stats = sb("stats", [P, B, 6])
        mv = sb("mv", [P, B, 2])
        half_pow = sb("half_pow", [P, HB])
        ve = sb("ve", [P, B])
        rstd = sb("rstd", [P, B])
        x1 = sb("x1", [P, B, D])
        x1h = sb("x1h", [P, B * S], f32r)
        x1l = sb("x1l", [P, B * S], f32r)
        wh = sb("wh", [P, 2, M, F], f32r)
        wl = sb("wl", [P, 2, M, F], f32r)
        hh = sb("hh", [P, 2, HT], f32r)
        hl = sb("hl", [P, 2, HT], f32r)
        mix = sb("mix", [P, SH + 1, B * S])
        ea = sb("ea", [P, S])
        gq = sb("gq", [P, T, E])
        gm = sb("gm", [P, T])
        gs = sb("gs", [P, T])
        wt = sb("wt", [P, 2, T, B])
        wab = sb("wab", [P, 2, B])
        kind_f = sb("kind_f", [P, B])
        gp = sb("gp", [P, B])
        hg = sb("hg", [P, P])
        nmax = sb("nmax", [P, 1])
        ge = sb("ge", [P, SH + 1])
        gsum = sb("gsum", [P, 1])
        grec = sb("grec", [P, 1])
        coef = sb("coef", [P, SH + 1])
        prod = sb("prod", [P, SH + 1, S])
        pair = sb("pair", [P, 2, S])
        comb = sb("comb", [P, 2, S])
        o_sb = sb("o_sb", [P, B, D])

        bank = [ctx.enter_context(nc.psum_tensor(f"bank{n}", [P, 512], f32)) for n in range(8)]
        h_ps = bank[0:2]
        acc = bank[2:4]
        t_ps = bank[4]
        w1_ps = bank[5]
        w2_ps = bank[6]
        x1_ps = bank[7]

        s_lang = sem("s_lang")
        s_langl = sem("s_langl")
        s_kind = sem("s_kind")
        s_kindp = sem("s_kindp")
        s_par = sem("s_par")
        s_gv = sem("s_gv")
        s_gate = sem("s_gate")
        s_x = [sem(f"s_x_half{h}") for h in range(NH)]
        s_w1 = [sem(f"s_w1_half{h}") for h in range(NH)]
        s_w2 = [sem(f"s_w2_half{h}") for h in range(NH)]
        s_raw = [sem(f"s_raw{m}") for m in range(M)]
        s_ident = sem("s_ident")
        s_langno = sem("s_langno")
        s_zero = sem("s_zero")
        s_onehot = sem("s_onehot")
        s_b1 = sem("s_b1")
        s_b1c = sem("s_b1c")
        s_pb = sem("s_pb")
        s_pbc = sem("s_pbc")
        s_xt = sem("s_xt")
        s_xtc = sem("s_xtc")
        s_h0 = sem("s_h0")
        s_h0r = sem("s_h0r")
        s_y = sem("s_y")
        s_xb = sem("s_xb")
        s_yc = sem("s_yc")
        s_stat = sem("s_stat")
        s_mv = sem("s_mv")
        s_rstd = sem("s_rstd")
        s_x1 = sem("s_x1")
        s_x1t = sem("s_x1t")
        s_x1h = sem("s_x1h")
        s_x1l = sem("s_x1l")
        s_wh = [sem(f"s_wh{m}") for m in range(M)]
        s_wl = [sem(f"s_wl{m}") for m in range(M)]
        s_mm1 = sem("s_mm1")
        s_hh = sem("s_hh")
        s_hl = sem("s_hl")
        s_mm2 = sem("s_mm2")
        s_out1 = sem("s_out1")
        s_gvq = sem("s_gvq")
        s_gve = sem("s_gve")
        s_gvp = sem("s_gvp")
        s_wab = sem("s_wab")
        s_ea = sem("s_ea")
        s_eo = sem("s_eo")
        s_gp = sem("s_gp")
        s_gpc = sem("s_gpc")
        s_ga = sem("s_ga")
        s_hg = sem("s_hg")
        s_gb = sem("s_gb")
        s_max = sem("s_max")
        s_ge = sem("s_ge")
        s_coef = sem("s_coef")
        s_comb = sem("s_comb")
        s_ot = sem("s_ot")
        s_o = sem("s_o")
        s_store = sem("s_store")
        s_dve = sem("s_dve")
        s_pool = sem("s_pool")

        def half(h):
            return slice(h * HB, (h + 1) * HB)

        def cols(h):
            return slice(h * HT, (h + 1) * HT)

        units = [(h, m, c) for h in range(NH) for m in range(SH) for c in range(FC)]

        block = ctx.enter_context(nc.Block())

        @block.sync
        def _(sp):
            sp.dma_start(lang_row[:, :], language.rearrange("(a b) -> a b", a=1)).then_inc(s_lang, 16)
            for h in range(NH):
                sp.dma_start(x_in[:, half(h), :],
                             x[half(h), :, :].rearrange("b s d -> s b d")).then_inc(s_x[h], 16)
            sp.wait_ge(s_lang, 16)
            for h in range(NH):
                for j in range(HB):
                    b = h * HB + j
                    lang = sp.value_load(lang_row[0:1, b:b + 1], min_val=0, max_val=L - 1)
                    sp.dma_start(W1s[:, b, :],
                                 W1[bass.ds(lang, 1), :, :].rearrange("l d a -> (l d) a")).then_inc(s_w1[h], 16)
                    sp.dma_start(W2s[A * j:A * j + A, h, :],
                                 W2[bass.ds(lang, 1), :, :].rearrange("l a d -> (l a) d")).then_inc(s_w2[h], 16)
            for e in range(E):
                sp.dma_start(w_raw[:, 0, SH + e, :], expert_wi[e, :, :]).then_inc(s_raw[SH + e], 16)
                sp.dma_start(w_raw[:, 1, SH + e, :].rearrange("p (c d) -> p c d", d=D),
                             expert_wo[e, :, :].rearrange("(c p) d -> p c d", p=P)).then_inc(s_raw[SH + e], 16)
            for b in range(B):
                sp.wait_ge(s_o, b + 1)
                sp.dma_start(out[b, :, :], o_sb[:, b, :]).then_inc(s_store, 16)
            sp.wait_ge(s_store, 16 * B)

        @block.gpsimd
        def _(pool):
            chain = [0]

            def link(ins):
                chain[0] += 1
                ins.then_inc(s_pool, 1)
                pool.wait_ge(s_pool, chain[0])

            nc.gpsimd.iota(lang_no[:, :], pattern=[[0, 1]], base=0, channel_multiplier=1,
                           allow_small_or_imprecise_dtypes=True).then_inc(s_langno, 1)
            link(nc.gpsimd.memset(ident[:, :], 0.0))
            nc.gpsimd.affine_select(out=ident[:, :], in_=ident[:, :], compare_op=ALU.not_equal, fill=1.0,
                                    base=0, pattern=[[-1, P]], channel_multiplier=1).then_inc(s_ident, 1)
            nc.gpsimd.memset(hbd[:, :, :], 0.0).then_inc(s_zero, 1)
            link(nc.gpsimd.memset(half_pow[:, :], -0.5))

            def residuals(h):
                pool.wait_ge(s_x[h], 16)
                pool.wait_ge(s_pbc, HB * (h + 1))
                nc.gpsimd.tensor_tensor(x_b2[:, half(h), :], x_in[:, half(h), :], par[:, half(h), 0, :],
                                        ALU.add).then_inc(s_xb, 1)
                nc.gpsimd.tensor_tensor(x_beta[:, half(h), :], x_in[:, half(h), :], par[:, half(h), 2, :],
                                        ALU.add).then_inc(s_xb, 1)

            def inverse_deviation(h):
                pool.wait_ge(s_mv, HB * (h + 1))
                link(nc.gpsimd.tensor_scalar(ve[:, half(h)], mv[:, half(h), 1], EPS, None, ALU.add))
                nc.gpsimd.tensor_tensor(rstd[:, half(h)], ve[:, half(h)], half_pow[:, :],
                                        ALU.pow).then_inc(s_rstd, 1)

            def split(m, k):
                if k == 0:
                    pool.wait_ge(s_raw[m], 32)
                nc.gpsimd.tensor_copy(wh[:, k, m, :], w_raw[:, k, m, :]).then_inc(s_wh[m], 1)
                pool.wait_ge(s_wh[m], k + 1)
                nc.gpsimd.tensor_tensor(wl[:, k, m, :], w_raw[:, k, m, :], wh[:, k, m, :].bitcast(f32),
                                        ALU.subtract).then_inc(s_wl[m], 1)

            residuals(0)
            pool.wait_ge(s_kindp, 16)
            link(nc.gpsimd.tensor_copy(kind_f[:, :], kind_p[:, :]))
            pool.wait_ge(s_gvp, 1)
            for k in range(2):
                for t in range(T):
                    link(nc.gpsimd.tensor_scalar(wt[:, k, t, :], kind_f[:, :], float(t), gq[:, t, t + k:t + k + 1],
                                                 ALU.is_equal, ALU.mult))
            link(nc.gpsimd.tensor_tensor(wab[:, :, :], wt[:, :, 0, :], wt[:, :, 1, :], ALU.add))
            nc.gpsimd.tensor_tensor(wab[:, :, :], wab[:, :, :], wt[:, :, 2, :], ALU.add).then_inc(s_wab, 1)
            inverse_deviation(0)
            residuals(1)
            split(1, 0)
            split(1, 1)
            inverse_deviation(1)
            for m in range(2, M):
                split(m, 0)
                split(m, 1)

            def mixture(b):
                c = bass.ds(b * S, S)
                pool.wait_ge(s_coef, b + 1)
                nc.gpsimd.tensor_tensor(prod[:, :, :], mix[:, :, c],
                                        coef[:, :].unsqueeze(2).to_broadcast([P, SH + 1, S]),
                                        ALU.mult).then_inc(s_pool, 1)
                pool.wait_ge(s_pool, chain[0] + 2 * b + 1)
                nc.gpsimd.tensor_tensor(pair[:, :, :], prod[:, 0:2, :], prod[:, 2:4, :],
                                        ALU.add).then_inc(s_pool, 1)
                pool.wait_ge(s_pool, chain[0] + 2 * b + 2)

            mixture(0)
            nc.gpsimd.tensor_tensor(comb[:, 0, :], pair[:, 0, :], pair[:, 1, :], ALU.add).then_inc(s_comb, 1)
            with pool.Fori(1, B) as b:
                mixture(b)
                pool.wait_ge(s_ot, b)
                nc.gpsimd.tensor_tensor(comb[:, 0, :], pair[:, 0, :], pair[:, 1, :], ALU.add).then_inc(s_comb, 1)

        @block.scalar
        def _(act):
            act.dma_start(lang_l[:, :], language.rearrange("(a b) -> a b", a=1).to_broadcast([L, B])).then_inc(s_langl, 16)
            act.dma_start(b1_l[:, :, :], b1.rearrange("l (r a) -> l r a", r=1).to_broadcast([L, HB, A])).then_inc(s_par, 16)
            for n, v in enumerate((b2, gamma, beta)):
                act.dma_start(par_l[:, n, :], v).then_inc(s_par, 16)
            act.dma_start(gv[:, :, :].rearrange("p t e -> p (t e)"),
                          gate_vecs.rearrange("(o t) e -> o (t e)", o=1).to_broadcast([P, T * E])).then_inc(s_gv, 16)
            act.dma_start(kind_p[:, :], kind.rearrange("(a b) -> a b", a=1).to_broadcast([P, B])).then_inc(s_kindp, 16)
            act.dma_start(kind_row[:, :], kind.rearrange("(a b) -> a b", a=1)).then_inc(s_kind, 16)
            for m in range(SH):
                act.dma_start(w_raw[:, 0, m, :], share_wi[m, :, :]).then_inc(s_raw[m], 16)
                act.dma_start(w_raw[:, 1, m, :].rearrange("p (c d) -> p c d", d=D),
                              share_wo[m, :, :].rearrange("(c p) d -> p c d", p=P)).then_inc(s_raw[m], 16)
            act.dma_start(gw1[:, :, :], gate_w1.rearrange("(i p) d -> p i d", p=P)).then_inc(s_gate, 16)
            act.dma_start(gw2[:, :], gate_w2).then_inc(s_gate, 16)

            def copy_params(b):
                act.wait_ge(s_pb, b + 1)
                nc.scalar.activation(par[:, b, :, :].rearrange("p n d -> p (n d)"), bank[b % 4][:, 0:3 * D],
                                     ACT.Copy).then_inc(s_pbc, 1)

            def adapter_relu(h):
                act.wait_ge(s_h0, h + 1)
                act.wait_ge(s_b1c, 1)
                act.wait_ge(s_zero, 1)
                for j in range(HB):
                    rows = slice(A * j, A * j + A)
                    nc.scalar.activation(hbd[rows, h, j * S:(j + 1) * S], w1_ps[rows, j * S:(j + 1) * S], ACT.Relu,
                                         bias=b1_c[rows, h * HB + j:h * HB + j + 1]).then_inc(s_h0r, 1)

            def x1_high(h):
                act.wait_ge(s_x1t, h + 1)
                nc.scalar.activation(x1h[:, cols(h)], x1_ps[:, :], ACT.Copy).then_inc(s_x1h, 1)

            act.wait_ge(s_gvq, 1)
            nc.scalar.activation(gq[:, :, :], gq[:, :, :], ACT.Exp).then_inc(s_gve, 1)
            for b in range(HB):
                copy_params(b)
            adapter_relu(0)
            for b in range(HB, B):
                copy_params(b)
            act.wait_ge(s_raw[0], 32)
            for k in range(2):
                nc.scalar.activation(wh[:, k, 0, :], w_raw[:, k, 0, :], ACT.Copy).then_inc(s_wh[0], 1)
            adapter_relu(1)
            x1_high(0)

            def hidden_high(h_bank, mm1_done, mm2_done):
                act.wait_ge(s_mm1, mm1_done)
                if mm2_done is not None:
                    act.wait_ge(s_mm2, mm2_done)
                nc.scalar.activation(hh[:, h_bank, :], h_ps[h_bank][:, :], ACT.Relu).then_inc(s_hh, 1)

            def shared_out(n):
                h, m = divmod(n, SH)
                act.wait_ge(s_mm2, (n + 1) * FC)
                nc.scalar.activation(mix[:, 1 + m, cols(h)], acc[n % 2][:, :], ACT.Copy).then_inc(s_out1, 1)

            for u in range(UNITS):
                hidden_high(u % 2, u + 1, u - 1 if u >= 2 else None)
                if u == 4:
                    x1_high(1)
                if u % FC == 0 and u:
                    shared_out(u // FC - 1)

            def expert_a(b):
                act.wait_ge(s_mm2, UNITS + 2 * b + 1)
                if isinstance(b, int) and b == 0:
                    act.wait_ge(s_wab, 1)
                else:
                    act.wait_ge(s_eo, b)
                nc.scalar.activation(ea[:, :], acc[0][:, 0:S], ACT.Copy,
                                     scale=wab[:, 0, bass.ds(b, 1)]).then_inc(s_ea, 1)

            def gate_hidden(b):
                act.wait_ge(s_ga, b + 1)
                nc.scalar.activation(hg[:, :], w2_ps[:, 0:1].to_broadcast([P, P]), ACT.Relu,
                                     bias=gp[:, bass.ds(b, 1)]).then_inc(s_hg, 1)

            def gate_exp(b):
                act.wait_ge(s_max, b + 1)
                nc.scalar.activation(ge[:, :], w1_ps[:, 0:SH + 1], ACT.Exp, bias=nmax[:, :],
                                     accum_out=gsum[:, :]).then_inc(s_ge, 1)

            hidden_high(0, UNITS + 1, UNITS - 1)
            shared_out(NH * SH - 1)
            hidden_high(1, UNITS + 2, UNITS)
            expert_a(0)
            act.wait_ge(s_gp, 1)
            nc.scalar.activation(gp[:, :], w2_ps[:, 0:B], ACT.Copy).then_inc(s_gpc, 1)
            hidden_high(0, UNITS + 3, UNITS + 1)
            act.wait_ge(s_gpc, 1)
            with act.Fori(1, B - 1) as b:
                hidden_high(1, 2 * b + (UNITS + 2), 2 * b + UNITS)
                expert_a(b)
                gate_hidden(b - 1)
                hidden_high(0, 2 * b + (UNITS + 3), 2 * b + (UNITS + 1))
                gate_exp(b - 1)
            b = B - 1
            hidden_high(1, UNITS + 2 * b + 2, UNITS + 2 * b)
            expert_a(b)
            gate_hidden(b - 1)
            gate_exp(b - 1)
            gate_hidden(b)
            gate_exp(b)

        @block.vector
        def _(dve):
            chain = [0]

            def link(ins):
                chain[0] += 1
                ins.then_inc(s_dve, 1)
                dve.wait_ge(s_dve, chain[0])

            dve.wait_ge(s_langl, 16)
            link(nc.vector.tensor_copy(lang_f[:, :], lang_l[:, :]))
            dve.wait_ge(s_langno, 1)
            nc.vector.tensor_scalar(onehot[:, :], lang_f[:, :], lang_no[:, :], None, ALU.is_equal).then_inc(s_onehot, 1)
            dve.wait_ge(s_gv, 16)
            link(nc.vector.tensor_scalar(gv[:, :, :], gv[:, :, :], 10.0, None, ALU.mult))
            link(nc.vector.tensor_reduce(gm[:, :], gv[:, :, :], AX.X, ALU.max))
            nc.vector.tensor_tensor(gq[:, :, :], gv[:, :, :], gm[:, :].unsqueeze(2).to_broadcast([P, T, E]),
                                    ALU.subtract).then_inc(s_gvq, 1)
            dve.wait_ge(s_gve, 1)
            link(nc.vector.tensor_reduce(gs[:, :], gq[:, :, :], AX.X, ALU.add))
            link(nc.vector.reciprocal(gm[:, :], gs[:, :]))
            nc.vector.tensor_tensor(gq[:, :, :], gq[:, :, :], gm[:, :].unsqueeze(2).to_broadcast([P, T, E]),
                                    ALU.mult).then_inc(s_gvp, 1)
            dve.wait_ge(s_b1, 1)
            nc.vector.tensor_copy(b1_c[:, :], x1_ps[:, 0:B]).then_inc(s_b1c, 1)

            def x_transposed(h):
                dve.wait_ge(s_xt, h + 1)
                nc.vector.tensor_copy(xT[:, cols(h)], t_ps[:, :]).then_inc(s_xtc, 1)

            def norm_stats(h):
                dve.wait_ge(s_y, h + 1)
                dve.wait_ge(s_xb, 2 * h + 2)
                nc.vector.tensor_tensor(y[:, half(h), :].rearrange("p b d -> p (b d)"), w2_ps[:, :],
                                        x_b2[:, half(h), :].rearrange("p b d -> p (b d)"), ALU.add).then_inc(s_yc, 1)
                dve.wait_ge(s_yc, h + 1)
                for b in range(h * HB, (h + 1) * HB):
                    nc.vector.bn_stats(stats[:, b, :], y[:, b, :]).then_inc(s_stat, 1)
                for b in range(h * HB, (h + 1) * HB):
                    dve.wait_ge(s_stat, b + 1)
                    nc.vector.bn_aggr(mv[:, b, :], stats[:, b, :]).then_inc(s_mv, 1)

            def norm_apply(h):
                dve.wait_ge(s_rstd, h + 1)
                for b in range(h * HB, (h + 1) * HB):
                    ins = nc.vector.tensor_scalar(y[:, b, :], y[:, b, :], mv[:, b, 0:1], rstd[:, b:b + 1],
                                                  ALU.subtract, ALU.mult)
                link(ins)
                link(nc.vector.tensor_tensor(y[:, half(h), :], y[:, half(h), :], par[:, half(h), 1, :], ALU.mult))
                nc.vector.tensor_tensor(x1[:, half(h), :], y[:, half(h), :], x_beta[:, half(h), :],
                                        ALU.add).then_inc(s_x1, 1)

            def x1_low(h):
                dve.wait_ge(s_x1h, h + 1)
                nc.vector.tensor_tensor(x1l[:, cols(h)], x1_ps[:, :], x1h[:, cols(h)].bitcast(f32),
                                        ALU.subtract).then_inc(s_x1l, 1)

            x_transposed(0)
            x_transposed(1)
            norm_stats(0)
            norm_apply(0)
            x1_low(0)
            for k in range(2):
                dve.wait_ge(s_wh[0], k + 1)
                nc.vector.tensor_tensor(wl[:, k, 0, :], w_raw[:, k, 0, :], wh[:, k, 0, :].bitcast(f32),
                                        ALU.subtract).then_inc(s_wl[0], 1)

            def hidden_low(h_bank, done):
                dve.wait_ge(s_hh, done)
                nc.vector.scalar_tensor_tensor(out=hl[:, h_bank, :], in0=h_ps[h_bank][:, :], scalar=0.0,
                                               in1=hh[:, h_bank, :].bitcast(f32), op0=ALU.max,
                                               op1=ALU.subtract).then_inc(s_hl, 1)

            for u in range(UNITS):
                hidden_low(u % 2, u + 1)
                if u == 0:
                    norm_stats(1)
                if u == 2:
                    norm_apply(1)
                if u == 4:
                    x1_low(1)

            def expert_out(b):
                dve.wait_ge(s_mm2, 2 * b + (UNITS + 2))
                dve.wait_ge(s_ea, b + 1)
                nc.vector.scalar_tensor_tensor(out=mix[:, 0, bass.ds(b * S, S)], in0=acc[1][:, 0:S],
                                               scalar=wab[:, 1, bass.ds(b, 1)], in1=ea[:, :], op0=ALU.mult,
                                               op1=ALU.add).then_inc(s_eo, 1)

            def gate_max(b):
                dve.wait_ge(s_gb, b + 1)
                nc.vector.tensor_reduce(nmax[:, :], w1_ps[:, 0:SH + 1], AX.X, ALU.max, negate=True).then_inc(s_max, 1)

            def gate_weights(b):
                dve.wait_ge(s_ge, b + 1)
                nc.vector.reciprocal(grec[:, :], gsum[:, :]).then_inc(s_dve, 1)
                dve.wait_ge(s_dve, chain[0] + b + 1)
                if not (isinstance(b, int) and b == 0):
                    dve.wait_ge(s_comb, b)
                nc.vector.tensor_scalar(coef[:, :], ge[:, :], grec[:, :], None, ALU.mult).then_inc(s_coef, 1)

            def result(b):
                dve.wait_ge(s_ot, b + 1)
                nc.vector.tensor_tensor(o_sb[:, bass.ds(b, 1), :].rearrange("p b d -> p (b d)"), t_ps[:, 0:S],
                                        x1[:, bass.ds(b, 1), :].rearrange("p b d -> p (b d)"),
                                        ALU.add).then_inc(s_o, 1)

            hidden_low(0, UNITS + 1)
            hidden_low(1, UNITS + 2)
            hidden_low(0, UNITS + 3)
            expert_out(0)
            hidden_low(1, UNITS + 4)
            gate_max(0)
            hidden_low(0, UNITS + 5)
            gate_weights(0)
            with dve.Fori(2, B - 1) as b:
                expert_out(b - 1)
                hidden_low(1, 2 * b + (UNITS + 2))
                gate_max(b - 1)
                hidden_low(0, 2 * b + (UNITS + 3))
                gate_weights(b - 1)
                result(b - 2)
            b = B - 1
            expert_out(b - 1)
            hidden_low(1, UNITS + 2 * b + 2)
            gate_max(b - 1)
            gate_weights(b - 1)
            result(b - 2)
            expert_out(b)
            gate_max(b)
            gate_weights(b)
            result(b - 1)
            result(b)

        @block.tensor
        def _(pe):
            def transpose_x(h):
                pe.wait_ge(s_x[h], 16)
                if h:
                    pe.wait_ge(s_xtc, h)
                for j in range(HB):
                    mm = nc.tensor.transpose(t_ps[:, j * S:(j + 1) * S], x_in[:, h * HB + j, :], ident[:, :])
                mm.then_inc(s_xt, 1)

            def adapter_in(h):
                pe.wait_ge(s_xtc, h + 1)
                pe.wait_ge(s_w1[h], 16 * HB)
                if h:
                    pe.wait_ge(s_h0r, HB * h)
                nc.tensor.matmul(w1_ps[:, :], W1s[:, half(h), :], xT[:, cols(h)],
                                 start=True, stop=True).then_inc(s_h0, 1)

            def adapter_out(h):
                pe.wait_ge(s_w2[h], 16 * HB)
                pe.wait_ge(s_h0r, HB * (h + 1))
                if h:
                    pe.wait_ge(s_yc, h)
                for j in range(HB):
                    mm = nc.tensor.matmul(w2_ps[:, j * D:(j + 1) * D], hbd[:, h, j * S:(j + 1) * S], W2s[:, h, :],
                                          start=True, stop=True)
                mm.then_inc(s_y, 1)

            def params(b):
                if b >= 4:
                    pe.wait_ge(s_pbc, b - 3)
                nc.tensor.matmul(bank[b % 4][:, 0:3 * D], onehot[:, b:b + 1].to_broadcast([L, P]),
                                 par_l[:, :, :].rearrange("l n d -> l (n d)"), start=True, stop=True).then_inc(s_pb, 1)

            def transpose_x1(h):
                pe.wait_ge(s_x1, h + 1)
                pe.wait_ge(s_x1l, h) if h else pe.wait_ge(s_b1c, 1)
                for j in range(HB):
                    mm = nc.tensor.transpose(x1_ps[:, j * S:(j + 1) * S], x1[:, h * HB + j, :], ident[:, :])
                mm.then_inc(s_x1t, 1)

            pe.wait_ge(s_ident, 1)
            transpose_x(0)
            pe.wait_ge(s_onehot, 1)
            pe.wait_ge(s_par, 64)
            nc.tensor.matmul(x1_ps[:, 0:B], b1_l[:, :, :].rearrange("l r a -> l (r a)"), onehot[:, :],
                             start=True, stop=True).then_inc(s_b1, 1)
            for b in range(HB):
                params(b)
            adapter_in(0)
            transpose_x(1)
            for b in range(HB, B):
                params(b)
            adapter_out(0)
            adapter_in(1)
            adapter_out(1)
            transpose_x1(0)

            def first_product(dst, m, c, hi, lo):
                w = slice(c * P, (c + 1) * P)
                nc.tensor.matmul(dst, wh[:, 0, m, w], hi, start=True, stop=False)
                nc.tensor.matmul(dst, wl[:, 0, m, w], hi, start=False, stop=False)
                return nc.tensor.matmul(dst, wh[:, 0, m, w], lo, start=False, stop=True)

            def shared_first(u):
                h, m, c = units[u]
                if c == 0:
                    pe.wait_ge(s_wh[m], 2)
                    pe.wait_ge(s_wl[m], 2)
                if m == 0 and c == 0:
                    pe.wait_ge(s_x1h, h + 1)
                    pe.wait_ge(s_x1l, h + 1)
                if u < 2:
                    pe.wait_ge(s_pbc, B)
                else:
                    pe.wait_ge(s_hl, u - 1)
                first_product(h_ps[u % 2][:, :], m, c, x1h[:, cols(h)], x1l[:, cols(h)]).then_inc(s_mm1, 1)

            def shared_second(u):
                h, m, c = units[u]
                n = u // FC
                w = slice(c * P, (c + 1) * P)
                dst = acc[n % 2][:, :]
                pe.wait_ge(s_hh, u + 1)
                if c == 0 and n >= 2:
                    pe.wait_ge(s_out1, n - 1)
                nc.tensor.matmul(dst, wh[:, 1, m, w], hh[:, u % 2, :], start=(c == 0), stop=False)
                nc.tensor.matmul(dst, wl[:, 1, m, w], hh[:, u % 2, :], start=False, stop=False)
                pe.wait_ge(s_hl, u + 1)
                nc.tensor.matmul(dst, wh[:, 1, m, w], hl[:, u % 2, :], start=False,
                                 stop=(c == FC - 1)).then_inc(s_mm2, 1)

            shared_first(0)
            for u in range(UNITS):
                if u + 1 < UNITS:
                    if u == 3:
                        transpose_x1(1)
                    shared_first(u + 1)
                    shared_second(u)

            def by_type(t, body):
                for v in range(T):
                    with pe.If(t == v):
                        body(v)

            def expert_first(b, k, t):
                hi, lo = (v[:, bass.ds(b * S, S)] for v in (x1h, x1l))
                pe.wait_ge(s_hl, 2 * b + (UNITS + k - 1))

                def body(v):
                    for c in range(FC):
                        mm = first_product(h_ps[k][:, c * S:(c + 1) * S], SH + v + k, c, hi, lo)
                    mm.then_inc(s_mm1, 1)

                by_type(t, body)

            def expert_second(b, k, t):
                dst = acc[k][:, 0:S]
                pe.wait_ge(s_hh, 2 * b + (UNITS + k + 1))
                if isinstance(b, int) and b == 0:
                    pe.wait_ge(s_out1, NH * SH - 1 + k)
                else:
                    pe.wait_ge((s_ea, s_eo)[k], b)

                def body(v):
                    m = SH + v + k
                    for c in range(FC):
                        w = slice(c * P, (c + 1) * P)
                        nc.tensor.matmul(dst, wh[:, 1, m, w], hh[:, k, c * S:(c + 1) * S], start=(c == 0), stop=False)
                        nc.tensor.matmul(dst, wl[:, 1, m, w], hh[:, k, c * S:(c + 1) * S], start=False, stop=False)
                    pe.wait_ge(s_hl, 2 * b + (UNITS + k + 1))
                    for c in range(FC):
                        w = slice(c * P, (c + 1) * P)
                        mm = nc.tensor.matmul(dst, wh[:, 1, m, w], hl[:, k, c * S:(c + 1) * S], start=False,
                                              stop=(c == FC - 1))
                    mm.then_inc(s_mm2, 1)

                by_type(t, body)

            def type_of(b):
                return pe.value_load(kind_row[0:1, bass.ds(b, 1)], min_val=0, max_val=T - 1)

            def gate_first(b):
                pe.wait_ge(s_eo, b + 1)
                nc.tensor.matmul(w2_ps[:, 0:1], gw1[:, 0, :], mix[:, 0, bass.ds(b * S, 1)],
                                 start=True, stop=True).then_inc(s_ga, 1)

            def gate_logits(b):
                pe.wait_ge(s_hg, b + 1)
                nc.tensor.matmul(w1_ps[:, 0:SH + 1], hg[:, :], gw2[:, :], start=True, stop=True).then_inc(s_gb, 1)

            def transpose_out(b):
                pe.wait_ge(s_comb, b + 1)
                if not (isinstance(b, int) and b == 0):
                    pe.wait_ge(s_o, b)
                nc.tensor.transpose(t_ps[:, 0:S], comb[:, 0, :], ident[:, :]).then_inc(s_ot, 1)

            for m in range(SH, M):
                pe.wait_ge(s_wl[m], 2)
            pe.wait_ge(s_kind, 16)
            t0 = type_of(0)
            expert_first(0, 0, t0)
            shared_second(UNITS - 1)
            expert_first(0, 1, t0)
            expert_second(0, 0, t0)
            pe.wait_ge(s_gate, 32)
            pe.wait_ge(s_out1, NH * SH)
            for i in range(1, SH + 1):
                mm = nc.tensor.matmul(w2_ps[:, 0:B], gw1[:, i, :], mix[:, i, 0:B * S:S], start=(i == 1), stop=(i == SH))
            mm.then_inc(s_gp, 1)
            t1 = type_of(1)
            expert_first(1, 0, t1)
            expert_second(0, 1, t0)
            expert_first(1, 1, t1)
            expert_second(1, 0, t1)
            pe.wait_ge(s_gpc, 1)
            gate_first(0)
            t2 = type_of(2)
            expert_first(2, 0, t2)
            gate_logits(0)
            expert_second(1, 1, t1)
            with pe.Fori(2, B - 1) as b:
                t = type_of(b)
                expert_first(b, 1, t)
                expert_second(b, 0, t)
                gate_first(b - 1)
                tn = type_of(b + 1)
                expert_first(b + 1, 0, tn)
                gate_logits(b - 1)
                expert_second(b, 1, t)
                transpose_out(b - 2)
            b = B - 1
            t = type_of(b)
            expert_first(b, 1, t)
            expert_second(b, 0, t)
            gate_first(b - 1)
            gate_logits(b - 1)
            expert_second(b, 1, t)
            transpose_out(b - 2)
            gate_first(b)
            gate_logits(b)
            transpose_out(b - 1)
            transpose_out(b)


_INS = ['x', 'itok_B_0_8', 'itok_B_0_2', 'L0_cond_W1', 'L0_cond_b1', 'L0_cond_W2', 'L0_cond_b2', 'L0_cond_gamma',
        'L0_cond_beta', 'L1_cond_expert_wi', 'L1_cond_expert_wo', 'L1_cond_share_wi', 'L1_cond_share_wo',
        'L1_cond_gate_vecs', 'L1_cond_gate_w1', 'L1_cond_gate_w2']


def kernel(**inputs):
    import numpy as _np
    import concourse.bacc as _bacc
    from concourse import mybir as _mybir
    from concourse.bass_utils import run_bass_kernel_spmd as _run

    nc = _bacc.Bacc("TRN2", target_bir_lowering=False, num_devices=1)
    arrays, args = {}, []
    for name in _INS:
        a = _np.ascontiguousarray(inputs[name])
        arrays[f"in_{name}_dram"] = a
        args.append(nc.dram_tensor(f"in_{name}_dram", a.shape, _mybir.dt.from_np(a.dtype), kind="ExternalInput").ap())
    shape = inputs['x'].shape
    args.append(nc.dram_tensor("out_0_dram", shape, _mybir.dt.from_np(_np.dtype('float32')),
                               kind="ExternalOutput").ap())
    conditional_residual_mlps(nc, *args)
    r = _run(nc, [arrays], core_ids=[0])
    return r.results[0]["out_0_dram"]
```

```python
from contextlib import ExitStack

import concourse.bass as bass
from concourse import mybir



def conditional_residual_mlps(
    nc: bass.Bass,
    x: bass.AP,
    language: bass.AP,
    kind: bass.AP,
    W1: bass.AP,
    b1: bass.AP,
    W2: bass.AP,
    b2: bass.AP,
    gamma: bass.AP,
    beta: bass.AP,
    expert_wi: bass.AP,
    expert_wo: bass.AP,
    share_wi: bass.AP,
    share_wo: bass.AP,
    gate_vecs: bass.AP,
    gate_w1: bass.AP,
    gate_w2: bass.AP,
    out: bass.AP,
):
    f32 = mybir.dt.float32
    f32r = mybir.dt.float32r
    i32 = mybir.dt.int32
    ALU = mybir.AluOpType
    ACT = mybir.ActivationFunctionType
    AX = mybir.AxisListType

    B, S, D = x.shape
    L, _, A = W1.shape
    E, _, F = expert_wi.shape
    SH = share_wi.shape[0]
    T = gate_vecs.shape[0]
    G = SH + 1
    P = 128
    HB = P // A
    NH = B // HB
    HT = HB * S
    FC = F // P
    M = SH + E
    EPS = 1e-5
    assert S == P and D == P and HT == 512 and E == T + 1 and NH == 2 and FC == 4

    ORDER = [[0, 1, 2, 3, 4, 5, 6], [3, 4, 5, 6, 0, 1, 2]]
    RUNS = [(h, m) for h in range(NH) for m in ORDER[h]]
    UNITS = [(r, c) for r in range(len(RUNS)) for c in range(FC)]
    LAST = len(RUNS) - 1
    HALF_RUNS = M
    GATE = 3

    ctx = ExitStack()
    with ctx:
        def sb(name, shape, dt=f32):
            return ctx.enter_context(nc.sbuf_tensor(name, shape, dt))

        def sem(name):
            return ctx.enter_context(nc.semaphore(name))

        x_in = sb("x_in", [P, B, D])
        lang_p = sb("lang_p", [P, B], i32)
        kind_p = sb("kind_p", [P, B], i32)
        W1s = sb("W1s", [P, B, A])
        W2s = sb("W2s", [P, NH, D])
        b1_l = sb("b1_l", [L, HB, A])
        par_l = sb("par_l", [L, 3, D])
        gv = sb("gv", [P, T, E])
        gw1 = sb("gw1", [P, G, D])
        gw2 = sb("gw2", [P, G])
        w_raw = sb("w_raw", [P, 2, M, F])
        ident = sb("ident", [P, P])
        ones = sb("ones", [P, P])
        lang_no = sb("lang_no", [L, 1])
        lang_f = sb("lang_f", [L, B])
        onehot = sb("onehot", [L, B])
        b1_c = sb("b1_c", [P, B])
        par = sb("par", [P, B, 2, D])
        xT = sb("xT", [P, B * S])
        hbd = sb("hbd", [P, NH, HT])
        x_beta = sb("x_beta", [P, B, D])
        yg = sb("yg", [P, B, D])
        stats = sb("stats", [P, B, 6])
        mv = sb("mv", [P, B, 2])
        minus_half = sb("minus_half", [P, HB])
        ve = sb("ve", [P, B])
        rstd = sb("rstd", [P, B])
        x1 = sb("x1", [P, B, D])
        x1h = sb("x1h", [P, B * S], f32r)
        x1l = sb("x1l", [P, B * S], f32r)
        wh = sb("wh", [P, 2, M, F], f32r)
        wl = sb("wl", [P, 2, M, F], f32r)
        hh = sb("hh", [P, 2, HT], f32r)
        hl = sb("hl", [P, 2, HT], f32r)
        mix = sb("mix", [P, G, B * S])
        gq = sb("gq", [P, T, E])
        gm = sb("gm", [P, T])
        gs = sb("gs", [P, T])
        kind_f = sb("kind_f", [P, B])
        wt = sb("wt", [P, 2, T, B])
        wexp = sb("wexp", [P, E, B])
        gprod = sb("gprod", [P, NH, HB, G])
        gmax = sb("gmax", [P, NH, HB])
        ge = sb("ge", [P, NH, HB, G])
        gsum = sb("gsum", [P, NH, HB])
        grec = sb("grec", [P, NH, HB])
        g = sb("g", [P, NH, HB, G])
        comb = sb("comb", [P, B, S])
        o_sb = sb("o_sb", [P, B, D])

        bank = [ctx.enter_context(nc.psum_tensor(f"bank{n}", [P, 512], f32)) for n in range(8)]
        h_ps = bank[0:2]
        acc = bank[2:4]
        xt_ps = bank[4]
        y_ps = [bank[6], bank[4]]
        w1_ps = bank[5]
        x1_ps = bank[7]
        t_ps = [bank[4], bank[6]]

        s_lang, s_kind, s_b1in, s_par, s_gv, s_gate = (
            sem(n) for n in ("s_lang", "s_kind", "s_b1in", "s_par", "s_gv", "s_gate"))
        s_x = [sem(f"s_x_half{h}") for h in range(NH)]
        s_w1 = [sem(f"s_w1_half{h}") for h in range(NH)]
        s_w2 = [sem(f"s_w2_half{h}") for h in range(NH)]
        s_wi = [sem(f"s_wi{m}") for m in range(M)]
        s_wo = [sem(f"s_wo{m}") for m in range(M)]
        s_ident = sem("s_ident")
        s_ones = sem("s_ones")
        s_langno = sem("s_langno")
        s_zero = sem("s_zero")
        s_onehot = sem("s_onehot")
        s_b1 = sem("s_b1")
        s_b1c = sem("s_b1c")
        s_pb = sem("s_pb")
        s_pbc = sem("s_pbc")
        s_xt = sem("s_xt")
        s_xtc = sem("s_xtc")
        s_h0 = sem("s_h0")
        s_h0a = [sem(f"s_h0a{h}") for h in range(NH)]
        s_y = sem("s_y")
        s_xb = sem("s_xb")
        s_stat = sem("s_stat")
        s_mv = sem("s_mv")
        s_rstd = sem("s_rstd")
        s_cent = sem("s_cent")
        s_x1 = sem("s_x1")
        s_x1t = sem("s_x1t")
        s_x1h = sem("s_x1h")
        s_x1l = sem("s_x1l")
        s_wh = [sem(f"s_wh{m}") for m in range(M)]
        s_wl = [sem(f"s_wl{m}") for m in range(M)]
        s_mm1 = sem("s_mm1")
        s_hh = sem("s_hh")
        s_hl = sem("s_hl")
        s_mm2 = sem("s_mm2")
        s_out = sem("s_out")
        s_gvq = sem("s_gvq")
        s_gve = sem("s_gve")
        s_gvp = sem("s_gvp")
        s_wexp = sem("s_wexp")
        s_ga = sem("s_ga")
        s_gp = sem("s_gp")
        s_gl = sem("s_gl")
        s_gd = sem("s_gd")
        s_ge = sem("s_ge")
        s_g = sem("s_g")
        s_comb = sem("s_comb")
        s_ot = sem("s_ot")
        s_o = sem("s_o")
        s_store = sem("s_store")
        s_dve = sem("s_dve")
        s_pool = sem("s_pool")

        def half(h):
            return slice(h * HB, (h + 1) * HB)

        def cols(h):
            return slice(h * HT, (h + 1) * HT)

        def seq(b):
            return slice(b * S, (b + 1) * S)

        def on_all(row):
            return row.rearrange("(a b) -> a b", a=1).to_broadcast([P, B])

        READS = [1 if m < SH else HB for _, m in RUNS]
        READS[LAST] = HB

        def reads_until(r):
            return sum(READS[:r + 1])

        block = ctx.enter_context(nc.Block())

        @block.sync
        def _(sp):
            sp.dma_start(lang_p[:, :], on_all(language)).then_inc(s_lang, 16)
            sp.dma_start(x_in[:, half(0), :], x[half(0), :, :].rearrange("b s d -> s b d")).then_inc(s_x[0], 16)

            def load_wi(m):
                src = share_wi[m, :, :] if m < SH else expert_wi[m - SH, :, :]
                sp.dma_start(w_raw[:, 0, m, :], src).then_inc(s_wi[m], 16)

            def load_wo(m):
                src = share_wo[m, :, :] if m < SH else expert_wo[m - SH, :, :]
                sp.dma_start(w_raw[:, 1, m, :].rearrange("p (c d) -> p c d", d=D),
                             src.rearrange("(c p) d -> p c d", p=P)).then_inc(s_wo[m], 16)

            def load_adapters(h):
                langs = [sp.value_load(lang_p[0:1, b:b + 1], min_val=0, max_val=L - 1)
                         for b in range(h * HB, (h + 1) * HB)]
                for j, lang in enumerate(langs):
                    sp.dma_start(W1s[:, h * HB + j, :],
                                 W1[bass.ds(lang, 1), :, :].rearrange("l d a -> (l d) a")).then_inc(s_w1[h], 16)
                for j, lang in enumerate(langs):
                    sp.dma_start(W2s[A * j:A * j + A, h, :],
                                 W2[bass.ds(lang, 1), :, :].rearrange("l a d -> (l a) d")).then_inc(s_w2[h], 16)

            sp.wait_ge(s_lang, 16)
            load_adapters(0)
            sp.dma_start(x_in[:, half(1), :], x[half(1), :, :].rearrange("b s d -> s b d")).then_inc(s_x[1], 16)
            load_wi(0)
            load_wo(0)
            load_adapters(1)
            for m in range(1, M):
                load_wi(m)
                load_wo(m)
            sp.dma_start(gw1[:, :, :], gate_w1.rearrange("(i p) d -> p i d", p=P)).then_inc(s_gate, 16)
            sp.dma_start(gw2[:, :], gate_w2).then_inc(s_gate, 16)
            for b in range(B):
                sp.wait_ge(s_o, b + 1)
                sp.dma_start(out[b, :, :], o_sb[:, b, :]).then_inc(s_store, 16)
            sp.wait_ge(s_store, 16 * B)

        @block.gpsimd
        def _(pool):
            chain = [0]

            def link(ins):
                chain[0] += 1
                ins.then_inc(s_pool, 1)
                pool.wait_ge(s_pool, chain[0])

            nc.gpsimd.iota(lang_no[:, :], pattern=[[0, 1]], base=0, channel_multiplier=1,
                           allow_small_or_imprecise_dtypes=True).then_inc(s_langno, 1)
            link(nc.gpsimd.memset(ident[:, :], 0.0))
            nc.gpsimd.affine_select(out=ident[:, :], in_=ident[:, :], compare_op=ALU.not_equal, fill=1.0,
                                    base=0, pattern=[[-1, P]], channel_multiplier=1).then_inc(s_ident, 1)
            pool.dma_start(gv[:, :, :].rearrange("p t e -> p (t e)"),
                           gate_vecs.rearrange("(o t) e -> o (t e)", o=1).to_broadcast([P, T * E])).then_inc(s_gv, 16)
            pool.dma_start(kind_p[:, :], on_all(kind)).then_inc(s_kind, 16)
            nc.gpsimd.memset(hbd[:, :, :], 0.0).then_inc(s_zero, 1)
            nc.gpsimd.memset(ones[:, :], 1.0).then_inc(s_ones, 1)
            link(nc.gpsimd.memset(minus_half[:, :], -0.5))

            def add_beta(h):
                pool.wait_ge(s_x[h], 16)
                pool.wait_ge(s_pbc, HB * (h + 1))
                nc.gpsimd.tensor_tensor(x_beta[:, half(h), :], x_in[:, half(h), :], par[:, half(h), 1, :],
                                        ALU.add).then_inc(s_xb, 1)

            def inverse_deviation(h):
                pool.wait_ge(s_mv, HB * (h + 1))
                link(nc.gpsimd.tensor_scalar(ve[:, half(h)], mv[:, half(h), 1], EPS, None, ALU.add))
                nc.gpsimd.tensor_tensor(rstd[:, half(h)], ve[:, half(h)], minus_half[:, :],
                                        ALU.pow).then_inc(s_rstd, 1)

            def weights_low(m):
                for k in range(2):
                    pool.wait_ge(s_wh[m], k + 1)
                    nc.gpsimd.tensor_tensor(wl[:, k, m, :], w_raw[:, k, m, :], wh[:, k, m, :].bitcast(f32),
                                            ALU.subtract).then_inc(s_wl[m], 1)

            add_beta(0)
            inverse_deviation(0)
            add_beta(1)
            inverse_deviation(1)
            weights_low(1)
            weights_low(2)
            pool.wait_ge(s_kind, 16)
            link(nc.gpsimd.tensor_copy(kind_f[:, :], kind_p[:, :]))
            pool.wait_ge(s_gvp, 1)
            for k in range(2):
                for t in range(T):
                    dst = wexp[:, E - 1 if k else 0, :] if t == (T - 1) * k else wt[:, k, t, :]
                    link(nc.gpsimd.tensor_scalar(dst, kind_f[:, :], float(t), gq[:, t, t + k:t + k + 1],
                                                 ALU.is_equal, ALU.mult))
            nc.gpsimd.tensor_tensor(wexp[:, 1:E - 1, :], wt[:, 0, 1:T, :], wt[:, 1, 0:T - 1, :],
                                    ALU.add).then_inc(s_wexp, 1)
            for m in range(SH, M):
                weights_low(m)

        @block.scalar
        def _(act):
            act.dma_start(b1_l[:, :, :], b1.rearrange("l (r a) -> l r a", r=1).to_broadcast([L, HB, A])).then_inc(s_b1in, 16)
            for n, v in enumerate((b2, gamma, beta)):
                act.dma_start(par_l[:, n, :], v).then_inc(s_par, 16)

            def copy_params(b):
                act.wait_ge(s_pb, b + 1)
                nc.scalar.activation(par[:, b, :, :].rearrange("p n d -> p (n d)"), bank[b % 4][:, 0:2 * D],
                                     ACT.Copy).then_inc(s_pbc, 1)

            def adapter_relu(h, js):
                act.wait_ge(s_h0, h + 1)
                act.wait_ge(s_b1c, 1)
                act.wait_ge(s_zero, 1)
                for j in js:
                    rows = slice(A * j, A * j + A)
                    nc.scalar.activation(hbd[rows, h, seq(j)], w1_ps[rows, seq(j)], ACT.Relu,
                                         bias=b1_c[rows, h * HB + j:h * HB + j + 1]).then_inc(s_h0a[h], 1)

            def x1_high(h):
                act.wait_ge(s_x1t, h + 1)
                nc.scalar.activation(x1h[:, cols(h)], x1_ps[:, :], ACT.Copy).then_inc(s_x1h, 1)

            def weights_high(m, k):
                act.wait_ge((s_wi, s_wo)[k][m], 16)
                nc.scalar.activation(wh[:, k, m, :], w_raw[:, k, m, :], ACT.Copy).then_inc(s_wh[m], 1)

            def hidden_high(u):
                act.wait_ge(s_mm1, u + 1)
                if u >= 2:
                    act.wait_ge(s_mm2, u - 1)
                nc.scalar.activation(hh[:, u % 2, :], h_ps[u % 2][:, :], ACT.Relu).then_inc(s_hh, 1)

            def shared_output(r):
                h, m = RUNS[r]
                act.wait_ge(s_mm2, (r + 1) * FC)
                act.wait_ge(s_out, reads_until(r - 1)) if r else None
                nc.scalar.activation(mix[:, 1 + m, cols(h)], acc[r % 2][:, :], ACT.Copy).then_inc(s_out, 1)

            def gate_exp(h):
                act.wait_ge(s_gd, h + 1)
                nc.scalar.activation(ge[:, h, :, :], ge[:, h, :, :], ACT.Exp).then_inc(s_ge, 1)

            for b in range(HB):
                copy_params(b)
            act.wait_ge(s_gvq, 1)
            nc.scalar.activation(gq[:, :, :], gq[:, :, :], ACT.Exp).then_inc(s_gve, 1)
            adapter_relu(0, (0, 1))
            for b in range(HB, B):
                copy_params(b)
            weights_high(0, 0)
            adapter_relu(1, range(HB))
            weights_high(0, 1)
            x1_high(0)
            for u, (r, c) in enumerate(UNITS):
                hidden_high(u)
                if u == 2:
                    x1_high(1)
                if r < M - 1 and c in (0, 1):
                    weights_high(r + 1, c)
                if c == 0 and r and RUNS[r - 1][1] < SH:
                    shared_output(r - 1)
                if u == HALF_RUNS * FC + GATE + 1:
                    gate_exp(0)
            gate_exp(1)

        @block.vector
        def _(dve):
            chain = [0]

            def link(ins):
                chain[0] += 1
                ins.then_inc(s_dve, 1)
                dve.wait_ge(s_dve, chain[0])

            dve.wait_ge(s_lang, 16)
            link(nc.vector.tensor_copy(lang_f[:, :], lang_p[0:L, :]))
            dve.wait_ge(s_langno, 1)
            nc.vector.tensor_scalar(onehot[:, :], lang_f[:, :], lang_no[:, :], None, ALU.is_equal).then_inc(s_onehot, 1)

            def x_transposed(h):
                dve.wait_ge(s_xt, h + 1)
                nc.vector.tensor_copy(xT[:, cols(h)], xt_ps[:, :]).then_inc(s_xtc, 1)

            def adapter_relu(h, js):
                dve.wait_ge(s_h0, h + 1)
                dve.wait_ge(s_zero, 1)
                for j in js:
                    rows = slice(A * j, A * j + A)
                    nc.vector.tensor_scalar(hbd[rows, h, seq(j)], w1_ps[rows, seq(j)],
                                            b1_c[rows, h * HB + j:h * HB + j + 1], 0.0, ALU.add,
                                            ALU.max).then_inc(s_h0a[h], 1)

            def norm_stats(h):
                dve.wait_ge(s_y, h + 1)
                for j in range(HB):
                    nc.vector.bn_stats(stats[:, h * HB + j, :], y_ps[h][:, seq(j)]).then_inc(s_stat, 1)
                for b in range(h * HB, (h + 1) * HB):
                    dve.wait_ge(s_stat, b + 1)
                    nc.vector.bn_aggr(mv[:, b, :], stats[:, b, :]).then_inc(s_mv, 1)
                for j in range(HB):
                    b = h * HB + j
                    dve.wait_ge(s_mv, b + 1)
                    dve.wait_ge(s_pbc, b + 1)
                    nc.vector.scalar_tensor_tensor(out=yg[:, b, :], in0=y_ps[h][:, seq(j)], scalar=mv[:, b, 0:1],
                                                   in1=par[:, b, 0, :], op0=ALU.subtract,
                                                   op1=ALU.mult).then_inc(s_cent, 1)

            def norm_apply(h):
                dve.wait_ge(s_rstd, h + 1)
                dve.wait_ge(s_xb, h + 1)
                for b in range(h * HB, (h + 1) * HB):
                    dve.wait_ge(s_cent, b + 1)
                    nc.vector.scalar_tensor_tensor(out=x1[:, b, :], in0=yg[:, b, :], scalar=rstd[:, b:b + 1],
                                                   in1=x_beta[:, b, :], op0=ALU.mult, op1=ALU.add).then_inc(s_x1, 1)

            def x1_low(h):
                dve.wait_ge(s_x1h, h + 1)
                nc.vector.tensor_tensor(x1l[:, cols(h)], x1_ps[:, :], x1h[:, cols(h)].bitcast(f32),
                                        ALU.subtract).then_inc(s_x1l, 1)

            def weights_low(m, k):
                dve.wait_ge(s_wh[m], k + 1)
                nc.vector.tensor_tensor(wl[:, k, m, :], w_raw[:, k, m, :], wh[:, k, m, :].bitcast(f32),
                                        ALU.subtract).then_inc(s_wl[m], 1)

            def hidden_low(u):
                dve.wait_ge(s_hh, u + 1)
                nc.vector.scalar_tensor_tensor(out=hl[:, u % 2, :], in0=h_ps[u % 2][:, :], scalar=0.0,
                                               in1=hh[:, u % 2, :].bitcast(f32), op0=ALU.max,
                                               op1=ALU.subtract).then_inc(s_hl, 1)

            def expert_output(r, j):
                h, m = RUNS[r]
                b = h * HB + j
                dst, src, w = mix[:, 0, seq(b)], acc[r % 2][:, seq(j)], wexp[:, m - SH, b:b + 1]
                if j == 0:
                    dve.wait_ge(s_mm2, (r + 1) * FC)
                    dve.wait_ge(s_out, reads_until(r - 1)) if r else None
                if m == SH:
                    dve.wait_ge(s_wexp, 1)
                    nc.vector.tensor_scalar(dst, src, w, None, ALU.mult).then_inc(s_out, 1)
                else:
                    nc.vector.scalar_tensor_tensor(out=dst, in0=src, scalar=w, in1=dst, op0=ALU.mult,
                                                   op1=ALU.add).then_inc(s_out, 1)

            def gate_products(h):
                dve.wait_ge(s_ga, h + 1)
                nc.vector.scalar_tensor_tensor(out=gprod[:, h, :, :],
                                               in0=w1_ps[:, 0:HB].unsqueeze(2).to_broadcast([P, HB, G]), scalar=0.0,
                                               in1=gw2[:, :].unsqueeze(1).to_broadcast([P, HB, G]), op0=ALU.max,
                                               op1=ALU.mult).then_inc(s_gp, 1)

            def gate_shift(h):
                dve.wait_ge(s_gl, h + 1)
                logits = x1_ps[:, 0:HB * G].rearrange("p (b g) -> p b g", g=G)
                link(nc.vector.tensor_reduce(gmax[:, h, :], logits, AX.X, ALU.max))
                nc.vector.tensor_tensor(ge[:, h, :, :], logits, gmax[:, h, :].unsqueeze(2).to_broadcast([P, HB, G]),
                                        ALU.subtract).then_inc(s_gd, 1)

            def gate_weights(h):
                dve.wait_ge(s_ge, h + 1)
                link(nc.vector.tensor_reduce(gsum[:, h, :], ge[:, h, :, :], AX.X, ALU.add))
                link(nc.vector.reciprocal(grec[:, h, :], gsum[:, h, :]))
                nc.vector.tensor_tensor(g[:, h, :, :], ge[:, h, :, :], grec[:, h, :].unsqueeze(2).to_broadcast([P, HB, G]),
                                        ALU.mult).then_inc(s_g, 1)
                dve.wait_ge(s_g, h + 1)

            def mixture(b, from_psum=None):
                h, j = divmod(b, HB)
                w = g[:, h, j, :]
                dst = comb[:, b, :]
                link(nc.vector.tensor_scalar(dst, mix[:, 0, seq(b)], w[:, 0:1], None, ALU.mult))
                for i in range(1, G):
                    ins = nc.vector.scalar_tensor_tensor(out=dst, in0=mix[:, i, seq(b)], scalar=w[:, i:i + 1], in1=dst,
                                                         op0=ALU.mult, op1=ALU.add)
                    if i < G - 1:
                        link(ins)
                ins.then_inc(s_comb, 1)

            def result(b):
                dve.wait_ge(s_ot, b + 1)
                nc.vector.tensor_tensor(o_sb[:, b, :], t_ps[b % 2][:, 0:S], x1[:, b, :], ALU.add).then_inc(s_o, 1)

            x_transposed(0)
            dve.wait_ge(s_b1, 1)
            nc.vector.tensor_copy(b1_c[:, :], x1_ps[:, 0:B]).then_inc(s_b1c, 1)
            dve.wait_ge(s_b1c, 1)
            dve.wait_ge(s_gv, 16)
            link(nc.vector.tensor_scalar(gv[:, :, :], gv[:, :, :], 10.0, None, ALU.mult))
            link(nc.vector.tensor_reduce(gm[:, :], gv[:, :, :], AX.X, ALU.max))
            nc.vector.tensor_tensor(gq[:, :, :], gv[:, :, :], gm[:, :].unsqueeze(2).to_broadcast([P, T, E]),
                                    ALU.subtract).then_inc(s_gvq, 1)
            adapter_relu(0, (2, 3))
            x_transposed(1)
            norm_stats(0)
            norm_apply(0)
            weights_low(0, 0)
            x1_low(0)
            weights_low(0, 1)
            for u, (r, c) in enumerate(UNITS):
                hidden_low(u)
                if u == 0:
                    norm_stats(1)
                if u == 1:
                    norm_apply(1)
                if u == 3:
                    x1_low(1)
                if u == 4:
                    dve.wait_ge(s_gve, 1)
                    link(nc.vector.tensor_reduce(gs[:, :], gq[:, :, :], AX.X, ALU.add))
                    link(nc.vector.reciprocal(gm[:, :], gs[:, :]))
                    nc.vector.tensor_tensor(gq[:, :, :], gq[:, :, :], gm[:, :].unsqueeze(2).to_broadcast([P, T, E]),
                                            ALU.mult).then_inc(s_gvp, 1)
                if r and RUNS[r - 1][1] >= SH and c in (0, 1):
                    for j in (2 * c, 2 * c + 1):
                        expert_output(r - 1, j)
                v = u - HALF_RUNS * FC - GATE
                if v == 0:
                    gate_products(0)
                if v == 1:
                    gate_shift(0)
                if v == 2:
                    gate_weights(0)
                if 3 <= v < 3 + HB:
                    mixture(v - 3)
                if 5 <= v < 5 + HB:
                    result(v - 5)
            dve.wait_ge(s_mm2, len(UNITS))
            nc.vector.tensor_copy(mix[:, G - 1, cols(1)][:, 0:HT:S], acc[LAST % 2][:, 0:HT:S]).then_inc(s_out, HB)
            gate_products(1)
            gate_shift(1)
            gate_weights(1)
            for b in range(HB, B):
                h, j = divmod(b, HB)
                w = g[:, h, j, :]
                dst = comb[:, b, :]
                link(nc.vector.tensor_scalar(dst, mix[:, 0, seq(b)], w[:, 0:1], None, ALU.mult))
                for i in range(1, G):
                    src = mix[:, i, seq(b)] if i < G - 1 else acc[LAST % 2][:, seq(j)]
                    ins = nc.vector.scalar_tensor_tensor(out=dst, in0=src, scalar=w[:, i:i + 1], in1=dst,
                                                         op0=ALU.mult, op1=ALU.add)
                    if i < G - 1:
                        link(ins)
                ins.then_inc(s_comb, 1)
                if b > HB:
                    result(b - 1)
            result(B - 1)

        @block.tensor
        def _(pe):
            def transpose_x(h):
                pe.wait_ge(s_x[h], 16)
                if h:
                    pe.wait_ge(s_xtc, h)
                for j in range(HB):
                    mm = nc.tensor.transpose(xt_ps[:, seq(j)], x_in[:, h * HB + j, :], ident[:, :])
                mm.then_inc(s_xt, 1)

            def adapter_in(h):
                pe.wait_ge(s_xtc, h + 1)
                pe.wait_ge(s_w1[h], 16 * HB)
                if h:
                    pe.wait_ge(s_h0a[h - 1], HB)
                nc.tensor.matmul(w1_ps[:, :], W1s[:, half(h), :], xT[:, cols(h)],
                                 start=True, stop=True).then_inc(s_h0, 1)

            def residual(h):
                if h:
                    pe.wait_ge(s_xtc, NH)
                nc.tensor.matmul(y_ps[h][:, :], ident[:, :], x_in[:, half(h), :], start=True, stop=False,
                                 skip_group_check=True)
                for j in range(HB):
                    nc.tensor.matmul(y_ps[h][:, seq(j)], onehot[:, h * HB + j:h * HB + j + 1].to_broadcast([L, P]),
                                     par_l[:, 0, :], start=False, stop=False, skip_group_check=True)

            def adapter_out(h):
                pe.wait_ge(s_w2[h], 16 * HB)
                pe.wait_ge(s_h0a[h], HB)
                for j in range(HB):
                    mm = nc.tensor.matmul(y_ps[h][:, seq(j)], hbd[:, h, seq(j)], W2s[:, h, :],
                                          start=False, stop=(j == HB - 1), skip_group_check=True)
                mm.then_inc(s_y, 1)

            def params(b):
                if b >= 4:
                    pe.wait_ge(s_pbc, b - 3)
                nc.tensor.matmul(bank[b % 4][:, 0:2 * D], onehot[:, b:b + 1].to_broadcast([L, P]),
                                 par_l[:, 1:3, :].rearrange("l n d -> l (n d)"), start=True, stop=True).then_inc(s_pb, 1)

            def transpose_x1(h):
                pe.wait_ge(s_x1l, h) if h else pe.wait_ge(s_b1c, 1)
                for j in range(HB):
                    pe.wait_ge(s_x1, h * HB + j + 1)
                    mm = nc.tensor.transpose(x1_ps[:, seq(j)], x1[:, h * HB + j, :], ident[:, :])
                mm.then_inc(s_x1t, 1)

            def first_product(u):
                r, c = UNITS[u]
                h, m = RUNS[r]
                if c == 0 and h == 0:
                    pe.wait_ge(s_wh[m], 2)
                    pe.wait_ge(s_wl[m], 2)
                if c == 0 and r == h * HALF_RUNS:
                    pe.wait_ge(s_x1h, h + 1)
                    pe.wait_ge(s_x1l, h + 1)
                if u < 2:
                    pe.wait_ge(s_pbc, B)
                else:
                    pe.wait_ge(s_hl, u - 1)
                dst, w = h_ps[u % 2][:, :], slice(c * P, (c + 1) * P)
                hi, lo = x1h[:, cols(h)], x1l[:, cols(h)]
                nc.tensor.matmul(dst, wh[:, 0, m, w], hi, start=True, stop=False)
                nc.tensor.matmul(dst, wl[:, 0, m, w], hi, start=False, stop=False)
                nc.tensor.matmul(dst, wh[:, 0, m, w], lo, start=False, stop=True).then_inc(s_mm1, 1)

            def second_product(u):
                r, c = UNITS[u]
                h, m = RUNS[r]
                dst, w = acc[r % 2][:, :], slice(c * P, (c + 1) * P)
                pe.wait_ge(s_hh, u + 1)
                if c == 0 and r >= 2:
                    pe.wait_ge(s_out, reads_until(r - 2))
                nc.tensor.matmul(dst, wh[:, 1, m, w], hh[:, u % 2, :], start=(c == 0), stop=False)
                nc.tensor.matmul(dst, wl[:, 1, m, w], hh[:, u % 2, :], start=False, stop=False)
                pe.wait_ge(s_hl, u + 1)
                nc.tensor.matmul(dst, wh[:, 1, m, w], hl[:, u % 2, :], start=False,
                                 stop=(c == FC - 1)).then_inc(s_mm2, 1)

            def gate_hidden(h, terms, first, last):
                for i in terms:
                    mm = nc.tensor.matmul(w1_ps[:, 0:HB], gw1[:, i, :], mix[:, i, cols(h)][:, 0:HT:S],
                                          start=first and i == terms[0], stop=last and i == terms[-1])
                if last:
                    mm.then_inc(s_ga, 1)

            def gate_logits(h):
                pe.wait_ge(s_gp, h + 1)
                nc.tensor.matmul(x1_ps[:, 0:HB * G], ones[:, :], gprod[:, h, :, :].rearrange("p b g -> p (b g)"),
                                 start=True, stop=True).then_inc(s_gl, 1)

            def transpose_result(b):
                pe.wait_ge(s_comb, b + 1)
                if b >= 2:
                    pe.wait_ge(s_o, b - 1)
                nc.tensor.transpose(t_ps[b % 2][:, 0:S], comb[:, b, :], ident[:, :]).then_inc(s_ot, 1)

            pe.wait_ge(s_ident, 1)
            transpose_x(0)
            pe.wait_ge(s_onehot, 1)
            pe.wait_ge(s_b1in, 16)
            nc.tensor.matmul(x1_ps[:, 0:B], b1_l[:, :, :].rearrange("l r a -> l (r a)"), onehot[:, :],
                             start=True, stop=True).then_inc(s_b1, 1)
            pe.wait_ge(s_par, 48)
            residual(0)
            for b in range(HB):
                params(b)
            adapter_in(0)
            transpose_x(1)
            adapter_out(0)
            for b in range(HB, B):
                params(b)
            adapter_in(1)
            residual(1)
            adapter_out(1)
            transpose_x1(0)
            first_product(0)
            for u, (r, c) in enumerate(UNITS):
                if u + 1 < len(UNITS):
                    first_product(u + 1)
                second_product(u)
                if u == 2:
                    transpose_x1(1)
                v = u - HALF_RUNS * FC - GATE
                if v == 0:
                    pe.wait_ge(s_gate, 32)
                    pe.wait_ge(s_ones, 1)
                    pe.wait_ge(s_out, reads_until(HALF_RUNS - 1))
                    gate_hidden(0, range(G), True, True)
                if v == 1:
                    gate_logits(0)
                if 4 <= v < 4 + HB:
                    transpose_result(v - 4)
                if u == LAST * FC + 2:
                    pe.wait_ge(s_gp, 1)
                    pe.wait_ge(s_out, reads_until(LAST - 1))
                    gate_hidden(1, range(G - 1), True, False)
            pe.wait_ge(s_out, reads_until(LAST))
            gate_hidden(1, range(G - 1, G), False, True)
            gate_logits(1)
            for b in range(HB, B):
                transpose_result(b)


_INS = ['x', 'itok_B_0_8', 'itok_B_0_2', 'L0_cond_W1', 'L0_cond_b1', 'L0_cond_W2', 'L0_cond_b2', 'L0_cond_gamma',
        'L0_cond_beta', 'L1_cond_expert_wi', 'L1_cond_expert_wo', 'L1_cond_share_wi', 'L1_cond_share_wo',
        'L1_cond_gate_vecs', 'L1_cond_gate_w1', 'L1_cond_gate_w2']


def kernel(**inputs):
    import numpy as _np
    import concourse.bacc as _bacc
    from concourse import mybir as _mybir
    from concourse.bass_utils import run_bass_kernel_spmd as _run

    nc = _bacc.Bacc("TRN2", target_bir_lowering=False, num_devices=1)
    arrays, args = {}, []
    for name in _INS:
        a = _np.ascontiguousarray(inputs[name])
        arrays[f"in_{name}_dram"] = a
        args.append(nc.dram_tensor(f"in_{name}_dram", a.shape, _mybir.dt.from_np(a.dtype), kind="ExternalInput").ap())
    shape = inputs['x'].shape
    args.append(nc.dram_tensor("out_0_dram", shape, _mybir.dt.from_np(_np.dtype('float32')),
                               kind="ExternalOutput").ap())
    conditional_residual_mlps(nc, *args)
    r = _run(nc, [arrays], core_ids=[0])
    return r.results[0]["out_0_dram"]
```

```python
from contextlib import ExitStack

import concourse.bass as bass
from concourse import mybir



def conditional_residual_mlps(
    nc: bass.Bass,
    x: bass.AP,
    language: bass.AP,
    kind: bass.AP,
    W1: bass.AP,
    b1: bass.AP,
    W2: bass.AP,
    b2: bass.AP,
    gamma: bass.AP,
    beta: bass.AP,
    expert_wi: bass.AP,
    expert_wo: bass.AP,
    share_wi: bass.AP,
    share_wo: bass.AP,
    gate_vecs: bass.AP,
    gate_w1: bass.AP,
    gate_w2: bass.AP,
    out: bass.AP,
):
    f32 = mybir.dt.float32
    f32r = mybir.dt.float32r
    i32 = mybir.dt.int32
    ALU = mybir.AluOpType
    ACT = mybir.ActivationFunctionType
    AX = mybir.AxisListType

    B, S, D = x.shape
    L, _, A = W1.shape
    E, _, F = expert_wi.shape
    SH = share_wi.shape[0]
    T = gate_vecs.shape[0]
    G = SH + 1
    P = 128
    HB = P // A
    NH = B // HB
    HT = HB * S
    FC = F // P
    M = SH + E
    EPS = 1e-5
    assert S == P and D == P and HT == 512 and E == T + 1 and NH == 2 and FC == 4

    ALL, PARTS = None, (0, 1)
    EXTRA, BASE, PR = 2, B, B // 2
    SLOTS = EXTRA + BASE
    RUNS = ([("shared", 0, m, ALL) for m in range(SH)]
            + [("extra", x) for x in range(EXTRA)] + [("base", k) for k in range(BASE)]
            + [("shared", 1, m, part) for part in PARTS for m in range(SH)])
    SETS, RING = SH + SLOTS, M - SH
    UNITS = [(r, c) for r in range(len(RUNS)) for c in range(FC)]
    FIRST_SLOT, END_SLOT = SH, SH + SLOTS
    LAST = len(RUNS) - 1
    GATE_RUN = LAST - SH
    WARM = 8
    NBUF = 3
    AHEAD = NBUF - 1
    PAIR = 2
    PAIRS = B // PAIR
    GATES = [END_SLOT * FC + 7, (GATE_RUN + 1) * FC + 1]
    BY_POOL = (0, 1)
    MIXTURE_AT = [[(4 + i, i % G, 2 + i // G) for i in range(2 * G)],
                  [(4, 0, HB), (5, 0, HB + 1), (6, 1, HB), (7, 1, HB + 1), (9, 2, HB), (10, 2, HB + 1)]]
    HIGH_AT = {3: [(2, 0)], 4: [(2, 1)], 7: [(3, 0)], 8: [(3, 1)], 9: [(4, 0)], 10: [(4, 1)],
               11: [(5, 0)], 12: [(5, 1)]}
    for w in range(SH + 3, SETS):
        HIGH_AT.update({(w - 3) * FC + 1: [(w, 0)], (w - 3) * FC + 3: [(w, 1)]})
    RESULTS = {10: 0, 12: 1}

    ctx = ExitStack()
    with ctx:
        def sb(name, shape, dt=f32):
            return ctx.enter_context(nc.sbuf_tensor(name, shape, dt))

        def sem(name):
            return ctx.enter_context(nc.semaphore(name))

        x_in = sb("x_in", [P, B, D])
        lang_p = sb("lang_p", [P, B], i32)
        kind_p = sb("kind_p", [P, B], i32)
        W1s = sb("W1s", [P, B, A])
        W2s = sb("W2s", [P, NH, D])
        b1_l = sb("b1_l", [L, HB, A])
        par_l = sb("par_l", [L, 3, D])
        gv = sb("gv", [P, T, E])
        gw1 = sb("gw1", [P, G, D])
        gw2 = sb("gw2", [P, G])
        w_raw = sb("w_raw", [P, 2, M, F])
        ident = sb("ident", [P, P])
        ones = sb("ones", [P, P])
        lang_no = sb("lang_no", [L, 1])
        one = sb("one", [1, 2])
        lang_f = sb("lang_f", [L, B])
        onehot = sb("onehot", [L, B])
        cols_c = sb("cols_c", [P, 3, B])
        warm = sb("warm", [P, HT], mybir.dt.bfloat16)
        xT = sb("xT", [P, B * S])
        hbd = sb("hbd", [P, NH, HT])
        xT_beta = sb("xT_beta", [P, B * S])
        z = sb("z", [P, B, D])
        stats = sb("stats", [P, B, 6])
        mv = sb("mv", [P, B, 2])
        minus_half = sb("minus_half", [P, PAIR])
        ve = sb("ve", [P, B])
        rstd = sb("rstd", [P, B])
        x1T = sb("x1T", [P, B * S])
        x1hl = sb("x1hl", [P, B, 2, S], f32r)
        xs = sb("xs", [P, B, 2, S], f32r)
        xe = sb("xe", [P, EXTRA, 2, S], f32r)
        wh = sb("wh", [P, 2, M, F], f32r)
        wl = sb("wl", [P, 2, M, F], f32r)
        hh = sb("hh", [P, NBUF, HT], f32r)
        hl = sb("hl", [P, NBUF, HT], f32r)
        mix = sb("mix", [P, G, B * S])
        gq = sb("gq", [P, T, E])
        gm = sb("gm", [P, T])
        gs = sb("gs", [P, T])
        kind_f = sb("kind_f", [P, B])
        seq_no = sb("seq_no", [P, B])
        key = sb("key", [P, B])
        sq = sb("sq", [P, B, B])
        sq2 = sb("sq2", [P, B, B])
        rank = sb("rank", [P, B])
        ts = sb("ts", [P, PR, 2])
        pd = sb("pd", [P, PR])
        tri = sb("tri", [P, PR, PR])
        before = sb("before", [P, PR])
        xr = sb("xr", [P, EXTRA, PR])
        xm = sb("xm", [P, EXTRA, PR])
        xu = sb("xu", [P, EXTRA, PR])
        xw = sb("xw", [P, EXTRA, PR])
        N_TAB = 2 * B + 2 * EXTRA
        tab = sb("tab", [P, N_TAB])
        tab_i = sb("tab_i", [P, N_TAB], i32)
        code = sb("code", [P, 2 * B + EXTRA * PR])
        picked = sb("picked", [P, 2 * T, 2 * B + EXTRA * PR])
        wslot = sb("wslot", [P, 2 * B + EXTRA * PR])
        es = sb("es", [P, B, S])
        ex = sb("ex", [P, EXTRA, S])
        gprod = sb("gprod", [P, NH, HB, G])
        gmax = sb("gmax", [P, NH, HB])
        ge = sb("ge", [P, NH, HB, G])
        gsum = sb("gsum", [P, NH, HB])
        grec = sb("grec", [P, NH, HB])
        g = sb("g", [P, NH, HB, G])
        prod = sb("prod", [P, G, S])
        prod2 = sb("prod2", [P, G // 2, S])
        prod1 = sb("prod1", [P, PAIR, S])
        comb = sb("comb", [P, B, S])
        o_sb = sb("o_sb", [P, B, D])

        bank = [ctx.enter_context(nc.psum_tensor(f"bank{n}", [P, 512], f32)) for n in range(8)]
        h_ps = bank[0:NBUF]
        b1_ps = bank[1]
        cols_ps = bank[0]
        acc = bank[3:5]
        xt_ps = [bank[5], bank[3]]
        w1_ps = bank[6]
        y_ps = [bank[7], bank[5]]
        zt_ps = [bank[1:3], [bank[6], bank[5]]]
        gh_ps = bank[6]
        gl_ps = gh_ps[:, P:]
        last_acc = bank[7]
        t_ps = [bank[5], bank[5], bank[0], bank[1]]

        s_lang, s_kind, s_b1in, s_par, s_gv, s_gate = (
            sem(n) for n in ("s_lang", "s_kind", "s_b1in", "s_par", "s_gv", "s_gate"))
        s_x = [sem(f"s_x_half{h}") for h in range(NH)]
        s_w1 = [sem(f"s_w1_half{h}") for h in range(NH)]
        s_w2 = [sem(f"s_w2_half{h}") for h in range(NH)]
        s_wi = [sem(f"s_wi{w}") for w in range(SETS)]
        s_wo = [sem(f"s_wo{w}") for w in range(SETS)]
        s_ident = sem("s_ident")
        s_gb = sem("s_gb")
        s_ones = sem("s_ones")
        s_langno = sem("s_langno")
        s_zero = sem("s_zero")
        s_onehot = sem("s_onehot")
        s_warm = sem("s_warm")
        s_one = sem("s_one")
        s_cols = sem("s_cols")
        s_colsc = sem("s_colsc")
        s_xt = sem("s_xt")
        s_xtc = sem("s_xtc")
        s_h0 = sem("s_h0")
        s_h0a = [sem(f"s_h0a{h}") for h in range(NH)]
        s_y = sem("s_y")
        s_xb = sem("s_xb")
        s_stat = sem("s_stat")
        s_mv = sem("s_mv")
        s_rstd = sem("s_rstd")
        s_z = sem("s_z")
        s_zt = sem("s_zt")
        s_x1 = sem("s_x1")
        s_x1h = sem("s_x1h")
        s_x1l = sem("s_x1l")
        s_wh = [sem(f"s_wh{w}") for w in range(SETS)]
        s_wl = [sem(f"s_wl{w}") for w in range(SETS)]
        s_mm1 = sem("s_mm1")
        s_hh = sem("s_hh")
        s_hl = sem("s_hl")
        s_mm2 = sem("s_mm2")
        s_out = sem("s_out")
        s_gvq = sem("s_gvq")
        s_gve = sem("s_gve")
        s_gvp = sem("s_gvp")
        s_seqno = sem("s_seqno")
        s_tab = sem("s_tab")
        s_wslot = sem("s_wslot")
        s_xs = [sem(f"s_xs_pair{p}") for p in range(PR)]
        s_xe = sem("s_xe")
        s_es_base = sem("s_es_base")
        s_es = sem("s_es")
        s_ret = sem("s_ret")
        s_ga = sem("s_ga")
        s_gp = sem("s_gp")
        s_gl = sem("s_gl")
        s_gd = sem("s_gd")
        s_ge = sem("s_ge")
        s_g = sem("s_g")
        s_comb = sem("s_comb")
        s_ot = sem("s_ot")
        s_o = sem("s_o")
        s_store = sem("s_store")
        s_part = sem("s_part")
        s_dve = sem("s_dve")
        s_pool = sem("s_pool")

        def half(h):
            return slice(h * HB, (h + 1) * HB)

        def cols(h):
            return slice(h * HT, (h + 1) * HT)

        def seq(b):
            return slice(b * S, (b + 1) * S)

        def pair(n):
            return slice(n * PAIR * S, (n + 1) * PAIR * S)

        def on_all(row):
            return row.rearrange("(a b) -> a b", a=1).to_broadcast([P, B])

        READS = [2 if run[0] == "base" else 1 for run in RUNS]

        def reads_until(r):
            return sum(READS[:r + 1])

        def set_of(r):
            return RUNS[r][2] if RUNS[r][0] == "shared" else r - FIRST_SLOT + SH

        def buf(w):
            return w if w < SH else SH + (w - SH) % RING

        def freed(w):
            return (FIRST_SLOT + w - SH - RING + 1) * FC

        def tokens(row, part):
            if part is ALL:
                return row
            n = S // len(PARTS)
            return row.rearrange("p (s t) -> p s t", t=S)[:, :, part * n:(part + 1) * n]

        def packed(row, r):
            run = RUNS[r]
            if run[0] == "shared":
                return row if run[3] is ALL else row[:, 0:HT // len(PARTS)].rearrange("p (s t) -> p s t", s=HB)
            return row[:, 0:S] if run[0] == "extra" else row[:, 0:2 * S].rearrange("p (s t) -> p s t", s=2)

        def x_of(r, lo):
            run = RUNS[r]
            if run[0] == "extra":
                return xe[:, run[1], lo, :]
            if run[0] == "base":
                return xs[:, run[1] // 2 * 2:run[1] // 2 * 2 + 2, lo, :]
            _, h, m, part = run
            n = S // len(PARTS)
            return x1hl[:, half(h), lo, slice(0, S) if part is ALL else slice(part * n, (part + 1) * n)]

        def acc_of(r):
            if RUNS[r][0] != "shared":
                return packed(acc[r % 2][:, :], r)
            _, h, m, part = RUNS[r]
            return tokens((last_acc if part is not ALL and m == SH - 1 else acc[r % 2])[:, :], part)

        results = list(RESULTS.values()) + list(range(len(RESULTS), PAIRS))

        block = ctx.enter_context(nc.Block())

        def load_adapters(engine, h, js):
            langs = []
            for j in js:
                lang = engine.value_load(lang_p[0:1, h * HB + j:h * HB + j + 1], min_val=0, max_val=L - 1)
                engine.dma_start(W1s[:, h * HB + j, :],
                                 W1[bass.ds(lang, 1), :, :].rearrange("l d a -> (l d) a")).then_inc(s_w1[h], 16)
                langs.append(lang)
            for j, lang in zip(js, langs):
                engine.dma_start(W2s[A * j:A * j + A, h, :],
                                 W2[bass.ds(lang, 1), :, :].rearrange("l a d -> (l a) d")).then_inc(s_w2[h], 16)

        @block.sync
        def _(sp):
            sp.dma_start(lang_p[:, :], on_all(language)).then_inc(s_lang, 16)
            sp.dma_start(x_in[:, half(0), :], x[half(0), :, :].rearrange("b s d -> s b d")).then_inc(s_x[0], 16)
            sp.dma_start(kind_p[:, :], on_all(kind)).then_inc(s_kind, 16)

            def load_wi(w, src):
                if w >= SH + RING:
                    sp.wait_ge(s_wl[w - RING], 2)
                sp.dma_start(w_raw[:, 0, buf(w), :], src).then_inc(s_wi[w], 16)

            def load_wo(w, src):
                sp.dma_start(w_raw[:, 1, buf(w), :].rearrange("p (c d) -> p c d", d=D),
                             src.rearrange("(c p) d -> p c d", p=P)).then_inc(s_wo[w], 16)

            def table(n, top):
                return sp.value_load(tab_i[0:1, n:n + 1], min_val=0, max_val=top)

            def load_slot(k):
                e = table(2 * B + k if k < EXTRA else B + k - EXTRA, E - 1)
                load_wi(SH + k, expert_wi[bass.ds(e, 1), :, :].rearrange("e d f -> (e d) f"))
                load_wo(SH + k, expert_wo[bass.ds(e, 1), :, :].rearrange("e f d -> (e f) d"))

            def put_back(p, order):
                sp.wait_ge(s_es, p + 1)
                for i in range(2):
                    sp.dma_start(mix[:, 0, :].rearrange("p (b s) -> p b s", s=S)[:, bass.ds(order[2 * p + i], 1), :],
                                 es[:, 2 * p + i:2 * p + i + 1, :]).then_inc(s_ret, 16)

            load_wi(0, share_wi[0, :, :])
            sp.wait_ge(s_lang, 16)
            load_adapters(sp, 0, (0, 1))
            load_wo(0, share_wo[0, :, :])
            load_adapters(sp, 1, range(HB))
            for m in range(1, SH):
                load_wi(m, share_wi[m, :, :])
                load_wo(m, share_wo[m, :, :])
            sp.wait_ge(s_tab, 1)
            order = [table(n, B - 1) for n in range(B)]
            sp.wait_ge(s_tab, 2)
            extras = [table(2 * B + EXTRA + k, B - 1) for k in range(EXTRA)]
            for k in range(RING):
                load_slot(k)
            sp.dma_start(gw1[:, :, :], gate_w1.rearrange("(i p) d -> p i d", p=P)).then_inc(s_gate, 16)
            sp.dma_start(gw2[:, :], gate_w2).then_inc(s_gate, 16)
            sp.wait_ge(s_x1h, PAIRS)
            sp.wait_ge(s_x1l, PAIRS)
            for k, b in enumerate(extras):
                sp.dma_start(xe[:, k:k + 1, :, :].bitcast(f32),
                             x1hl[:, :, :, :].bitcast(f32)[:, bass.ds(b, 1), :, :]).then_inc(s_xe, 16)
            for p in range(PR):
                for n in (2 * p, 2 * p + 1):
                    sp.dma_start(xs[:, n:n + 1, :, :].bitcast(f32),
                                 x1hl[:, :, :, :].bitcast(f32)[:, bass.ds(order[n], 1), :, :]).then_inc(s_xs[p], 16)
                if p:
                    load_slot(RING + p - 1)
            for k in range(RING + PR - 1, SLOTS):
                load_slot(k)
            for p in range(PR):
                put_back(p, order)
            for i, n in enumerate(results):
                b = slice(n * PAIR, (n + 1) * PAIR)
                sp.wait_ge(s_o, i + 1)
                sp.dma_start(out[b, :, :].rearrange("b s d -> s b d"), o_sb[:, b, :]).then_inc(s_store, 16)
            sp.wait_ge(s_store, 16 * PAIRS)

        @block.gpsimd
        def _(pool):
            chain = [0]

            def link(ins):
                chain[0] += 1
                ins.then_inc(s_pool, 1)
                pool.wait_ge(s_pool, chain[0])

            nc.gpsimd.iota(lang_no[:, :], pattern=[[0, 1]], base=0, channel_multiplier=1,
                           allow_small_or_imprecise_dtypes=True).then_inc(s_langno, 1)
            nc.gpsimd.iota(seq_no[:, :], pattern=[[1, B]], base=0, channel_multiplier=0,
                           allow_small_or_imprecise_dtypes=True).then_inc(s_seqno, 1)
            link(nc.gpsimd.memset(ident[:, :], 0.0))
            nc.gpsimd.affine_select(out=ident[:, :], in_=ident[:, :], compare_op=ALU.not_equal, fill=1.0,
                                    base=0, pattern=[[-1, P]], channel_multiplier=1).then_inc(s_ident, 1)
            pool.dma_start(par_l[:, 0, :], b2).then_inc(s_par, 16)
            pool.dma_start(par_l[:, 1, :], gamma).then_inc(s_gb, 16)
            pool.dma_start(par_l[:, 2, :], beta).then_inc(s_gb, 16)
            pool.dma_start(gv[:, :, :].rearrange("p t e -> p (t e)"),
                           gate_vecs.rearrange("(o t) e -> o (t e)", o=1).to_broadcast([P, T * E])).then_inc(s_gv, 16)
            link(nc.gpsimd.memset(minus_half[:, :], -0.5))

            def inverse_deviation(n):
                pool.wait_ge(s_mv, PAIR * (n + 1))
                b = slice(n * PAIR, (n + 1) * PAIR)
                link(nc.gpsimd.tensor_scalar(ve[:, b], mv[:, b, 1], EPS, None, ALU.add))
                nc.gpsimd.tensor_tensor(rstd[:, b], ve[:, b], minus_half[:, :], ALU.pow).then_inc(s_rstd, 1)

            def weights_low(w, ks=(0, 1)):
                for k in ks:
                    pool.wait_ge(s_wh[w], k + 1)
                    nc.gpsimd.tensor_tensor(wl[:, k, buf(w), :], w_raw[:, k, buf(w), :],
                                            wh[:, k, buf(w), :].bitcast(f32), ALU.subtract).then_inc(s_wl[w], 1)

            weights_low(0, (0,))
            inverse_deviation(0)
            inverse_deviation(1)
            weights_low(0, (1,))
            inverse_deviation(2)
            inverse_deviation(3)
            weights_low(1, (1,))
            weights_low(2)
            for w in range(SH, SETS):
                weights_low(w)
            pool.wait_ge(s_g, 1)
            for b in BY_POOL:
                link(nc.gpsimd.tensor_tensor(prod[:, :, :], mix[:, :, seq(b)],
                                             g[:, 0, b, :].unsqueeze(2).to_broadcast([P, G, S]), ALU.mult))
                link(nc.gpsimd.tensor_tensor(prod2[:, :, :], prod[:, 0:2, :], prod[:, 2:4, :], ALU.add))
                link(nc.gpsimd.tensor_tensor(prod1[:, 0, :], prod2[:, 0, :], prod2[:, 1, :], ALU.add))
                nc.gpsimd.tensor_tensor(comb[:, b, :], prod1[:, 0, :], x1T[:, seq(b)], ALU.add).then_inc(s_part, 1)
            pool.wait_ge(s_g, 2)
            n, b, j = PAIRS - 1, slice(B - PAIR, B), slice(HB - PAIR, HB)
            pool.wait_ge(s_out, reads_until(LAST - 2))
            link(nc.gpsimd.tensor_tensor(prod[:, :, :].rearrange("p (i b) s -> p i b s", i=2),
                                         mix[:, 0:2, pair(n)].rearrange("p i (b s) -> p i b s", s=S),
                                         g[:, 1, j, 0:2].rearrange("p b i -> p i b").unsqueeze(3)
                                         .to_broadcast([P, 2, PAIR, S]), ALU.mult))
            link(nc.gpsimd.tensor_tensor(prod2[:, :, :], prod[:, 0:2, :], prod[:, 2:4, :], ALU.add))
            link(nc.gpsimd.tensor_tensor(prod1[:, :, :], prod2[:, :, :],
                                         x1T[:, pair(n)].rearrange("p (b s) -> p b s", s=S), ALU.add))
            pool.wait_ge(s_out, reads_until(LAST - 1))
            link(nc.gpsimd.tensor_tensor(prod[:, 0:2, :], mix[:, 2, pair(n)].rearrange("p (b s) -> p b s", s=S),
                                         g[:, 1, j, 2:3].to_broadcast([P, PAIR, S]), ALU.mult))
            nc.gpsimd.tensor_tensor(comb[:, b, :], prod1[:, :, :], prod[:, 0:2, :], ALU.add).then_inc(s_part, 1)

        @block.scalar
        def _(act):
            act.wait_ge(s_one, 1)
            nc.scalar.activation(one[:, 1:2], one[:, 0:1], ACT.Exp)
            act.dma_start(b1_l[:, :, :], b1.rearrange("l (r a) -> l r a", r=1).to_broadcast([L, HB, A])).then_inc(s_b1in, 16)
            act.wait_ge(s_lang, 16)
            load_adapters(act, 0, (2, 3))
            act.dma_start(x_in[:, half(1), :], x[half(1), :, :].rearrange("b s d -> s b d")).then_inc(s_x[1], 16)

            def add_beta(h, js=range(HB)):
                act.wait_ge(s_colsc, 2)
                act.wait_ge(s_xtc, h + 1)
                for b in (h * HB + j for j in js):
                    nc.scalar.activation(xT_beta[:, seq(b)], xT[:, seq(b)], ACT.Identity,
                                         bias=cols_c[:, 2, b:b + 1]).then_inc(s_xb, 1)

            def adapter_relu(h, js):
                act.wait_ge(s_h0, h + 1)
                act.wait_ge(s_colsc, 1)
                act.wait_ge(s_zero, 1)
                for j in js:
                    rows = slice(A * j, A * j + A)
                    nc.scalar.activation(hbd[rows, h, seq(j)], w1_ps[rows, seq(j)], ACT.Relu,
                                         bias=cols_c[rows, 0, h * HB + j:h * HB + j + 1]).then_inc(s_h0a[h], 1)

            def x1_high(n):
                act.wait_ge(s_x1, n + 1)
                nc.scalar.activation(x1hl[:, n * PAIR:(n + 1) * PAIR, 0, :],
                                     x1T[:, pair(n)].rearrange("p (b s) -> p b s", s=S), ACT.Copy).then_inc(s_x1h, 1)

            def weights_high(w, k):
                act.wait_ge((s_wi, s_wo)[k][w], 16)
                if w >= SH + RING:
                    act.wait_ge(s_mm2, freed(w))
                nc.scalar.activation(wh[:, k, buf(w), :], w_raw[:, k, buf(w), :], ACT.Copy).then_inc(s_wh[w], 1)

            def hidden_high(u):
                act.wait_ge(s_mm1, u + 1)
                if u >= NBUF:
                    act.wait_ge(s_mm2, u - NBUF + 1)
                r = UNITS[u][0]
                nc.scalar.activation(packed(hh[:, u % NBUF, :], r), packed(h_ps[u % NBUF][:, :], r),
                                     ACT.Relu).then_inc(s_hh, 1)

            def shared_output(r):
                _, h, m, part = RUNS[r]
                act.wait_ge(s_mm2, (r + 1) * FC)
                if r:
                    act.wait_ge(s_out, reads_until(r - 1))
                dst, src = tokens(mix[:, 1 + m, cols(h)], part), acc_of(r)
                if r == GATE_RUN:
                    dst, src = dst[:, :, 0], src[:, :, 0]
                nc.scalar.activation(dst, src, ACT.Copy).then_inc(s_out, 1)

            def gate_exp(h):
                act.wait_ge(s_gd, h + 1)
                nc.scalar.activation(ge[:, h, :, :], ge[:, h, :, :], ACT.Exp).then_inc(s_ge, 1)

            def result(n):
                act.wait_ge(s_ot, results.index(n) + 1)
                nc.scalar.activation(o_sb[:, n * PAIR:(n + 1) * PAIR, :].rearrange("p b d -> p (b d)"),
                                     t_ps[n][:, 0:PAIR * S], ACT.Copy).then_inc(s_o, 1)

            weights_high(0, 0)
            adapter_relu(0, range(HB))
            add_beta(0)
            act.wait_ge(s_xt, 2)
            nc.scalar.activation(xT[:, cols(1)], xt_ps[1][:, :], ACT.Copy).then_inc(s_xtc, 1)
            weights_high(0, 1)
            x1_high(0)
            x1_high(1)
            adapter_relu(1, (0, 1))
            for u, (r, c) in enumerate(UNITS):
                hidden_high(u)
                if u < 2:
                    weights_high(1, u)
                if u in (2, 3):
                    add_beta(1, (2 * u - 4, 2 * u - 3))
                if u in (5, 6):
                    x1_high(u - 3)
                if u == 9:
                    act.wait_ge(s_gvq, 1)
                    nc.scalar.activation(gq[:, :, :], gq[:, :, :], ACT.Exp).then_inc(s_gve, 1)
                for w, k in HIGH_AT.get(u, ()):
                    weights_high(w, k)
                if r and RUNS[r - 1][0] == "shared" and c == (2 if r <= FIRST_SLOT else 1):
                    shared_output(r - 1)
                for h in range(NH):
                    if u == GATES[h] + 3:
                        gate_exp(h)
                if u - AHEAD - GATES[0] in RESULTS:
                    result(RESULTS[u - AHEAD - GATES[0]])
            result(2)

        @block.vector
        def _(dve):
            chain = [0]

            def link(ins):
                chain[0] += 1
                ins.then_inc(s_dve, 1)
                dve.wait_ge(s_dve, chain[0])

            nc.vector.memset(warm[:, :], 0.0).then_inc(s_warm, 1)
            nc.vector.memset(one[:, 0:1], 1.0).then_inc(s_one, 1)
            nc.vector.memset(hbd[:, :, :], 0.0).then_inc(s_zero, 1)
            nc.vector.memset(ones[:, :], 1.0).then_inc(s_ones, 1)
            dve.wait_ge(s_lang, 16)
            link(nc.vector.tensor_copy(lang_f[:, :], lang_p[0:L, :]))
            dve.wait_ge(s_langno, 1)
            nc.vector.tensor_scalar(onehot[:, :], lang_f[:, :], lang_no[:, :], None, ALU.is_equal).then_inc(s_onehot, 1)

            def tt(dst, a, b, op):
                link(nc.vector.tensor_tensor(dst, a, b, op))

            def stt(dst, a, scalar, b, op0, op1):
                link(nc.vector.scalar_tensor_tensor(out=dst, in0=a, scalar=scalar, in1=b, op0=op0, op1=op1))

            def total(dst, src):
                link(nc.vector.tensor_reduce(dst, src, AX.X, ALU.add))

            def across(v, n):
                return v.unsqueeze(1).to_broadcast([P, n, v.shape[1]])

            def down(v, n):
                return v.unsqueeze(2).to_broadcast([P, v.shape[1], n])

            no_p, no_x = seq_no[:, 0:PR], seq_no[:, 0:EXTRA]
            lower, upper = ts[:, :, 0], ts[:, :, 1]
            t_order, t_base = tab[:, 0:B], tab[:, B:2 * B]
            t_extra, t_extra_seq = tab[:, 2 * B:2 * B + EXTRA], tab[:, 2 * B + EXTRA:]

            def sort_by_type():
                dve.wait_ge(s_kind, 16)
                dve.wait_ge(s_seqno, 1)
                link(nc.vector.tensor_copy(kind_f[:, :], kind_p[:, :]))
                stt(key[:, :], kind_f[:, :], float(B), seq_no[:, :], ALU.mult, ALU.add)
                tt(sq[:, :, :], across(key[:, :], B), down(key[:, :], B), ALU.is_lt)
                total(rank[:, :], sq[:, :, :])
                tt(sq[:, :, :], across(rank[:, :], B), down(seq_no[:, :], B), ALU.is_equal)
                tt(sq2[:, :, :], sq[:, :, :], across(seq_no[:, :], B), ALU.mult)
                total(t_order, sq2[:, :, :])
                tt(sq[:, :, :], sq[:, :, :], across(kind_f[:, :], B), ALU.mult)
                total(ts[:, :, :].rearrange("p n i -> p (n i)"), sq[:, :, :])
                nc.vector.tensor_copy(tab_i[:, 0:B], t_order).then_inc(s_tab, 1)

            def slot_tables():
                tt(t_base.rearrange("p (n i) -> p n i", i=2), down(lower, 2), across(seq_no[:, 0:2], PR), ALU.add)
                tt(pd[:, :], upper, lower, ALU.subtract)
                tt(tri[:, :, :], across(no_p, PR), down(no_p, PR), ALU.is_lt)
                tt(tri[:, :, :], tri[:, :, :], across(pd[:, :], PR), ALU.mult)
                total(before[:, :], tri[:, :, :])
                tt(xr[:, :, :], down(no_x, PR), across(before[:, :], EXTRA), ALU.subtract)

            def extra_tables():
                tt(xm[:, :, :], xr[:, :, :], across(pd[:, :], EXTRA), ALU.is_lt)
                stt(xm[:, :, :], xr[:, :, :], 0.0, xm[:, :, :], ALU.is_ge, ALU.mult)
                stt(xu[:, :, :], xr[:, :, :], 2.0, across(lower, EXTRA), ALU.add, ALU.add)
                tt(xw[:, :, :], xu[:, :, :], xm[:, :, :], ALU.mult)

            def extra_tables_ends():
                total(t_extra, xw[:, :, :])
                tt(xw[:, :, :], xm[:, :, :], across(t_order.rearrange("p (n i) -> p n i", i=2)[:, :, 1], EXTRA), ALU.mult)
                total(t_extra_seq, xw[:, :, :])
                nc.vector.tensor_copy(tab_i[:, B:], tab[:, B:]).then_inc(s_tab, 1)

            def slot_weights():
                base, extra = code[:, 0:2 * B], code[:, 2 * B:]
                for e in range(2):
                    stt(base.rearrange("p (n e j) -> p n e j", e=2, j=2)[:, :, e, :], ts[:, :, :], float(E),
                        down(t_base.rearrange("p (n e) -> p n e", e=2)[:, :, e], 2), ALU.mult, ALU.add)
                stt(extra.rearrange("p (x n) -> p x n", n=PR), across(upper, EXTRA), float(E), xu[:, :, :],
                    ALU.mult, ALU.add)

            def slot_weights_ends():
                dve.wait_ge(s_gvp, 1)
                for t in range(T):
                    for k in range(2):
                        ins = nc.vector.tensor_scalar(picked[:, 2 * t + k, :], code[:, :], float(t * E + t + k),
                                                      gq[:, t, t + k:t + k + 1], ALU.is_equal, ALU.mult)
                link(ins)
                total(wslot[:, :], picked[:, :, :].rearrange("p n c -> p c n"))
                nc.vector.tensor_tensor(wslot[:, 2 * B:], wslot[:, 2 * B:], xm[:, :, :].rearrange("p x n -> p (x n)"),
                                        ALU.mult).then_inc(s_wslot, 1)

            def adapter_relu(h, js):
                dve.wait_ge(s_h0, h + 1)
                dve.wait_ge(s_zero, 1)
                for j in js:
                    rows = slice(A * j, A * j + A)
                    nc.vector.tensor_scalar(hbd[rows, h, seq(j)], w1_ps[rows, seq(j)],
                                            cols_c[rows, 0, h * HB + j:h * HB + j + 1], 0.0, ALU.add,
                                            ALU.max).then_inc(s_h0a[h], 1)

            def norm_stats(n):
                h = n // 2
                dve.wait_ge(s_y, h + 1)
                for b in range(n * PAIR, (n + 1) * PAIR):
                    nc.vector.bn_stats(stats[:, b, :], y_ps[h][:, seq(b - h * HB)]).then_inc(s_stat, 1)
                for b in range(n * PAIR, (n + 1) * PAIR):
                    dve.wait_ge(s_stat, b + 1)
                    nc.vector.bn_aggr(mv[:, b, :], stats[:, b, :]).then_inc(s_mv, 1)

            def norm_apply(n):
                h = n // 2
                dve.wait_ge(s_rstd, n + 1)
                for b in range(n * PAIR, (n + 1) * PAIR):
                    dve.wait_ge(s_mv, b + 1)
                    nc.vector.tensor_scalar(z[:, b, :], y_ps[h][:, seq(b - h * HB)], mv[:, b, 0:1], rstd[:, b:b + 1],
                                            ALU.subtract, ALU.mult).then_inc(s_z, 1)

            def x1_transposed(n):
                h, k = divmod(n, 2)
                dve.wait_ge(s_zt, n + 1)
                dve.wait_ge(s_xb, PAIR * (n + 1))
                for i in range(PAIR):
                    b = n * PAIR + i
                    ins = nc.vector.scalar_tensor_tensor(out=x1T[:, seq(b)], in0=zt_ps[h][k][:, seq(i)],
                                                         scalar=cols_c[:, 1, b:b + 1], in1=xT_beta[:, seq(b)],
                                                         op0=ALU.mult, op1=ALU.add)
                ins.then_inc(s_x1, 1)

            def x1_low(n):
                dve.wait_ge(s_x1h, n + 1)
                b = slice(n * PAIR, (n + 1) * PAIR)
                nc.vector.tensor_tensor(x1hl[:, b, 1, :], x1T[:, pair(n)].rearrange("p (b s) -> p b s", s=S),
                                        x1hl[:, b, 0, :].bitcast(f32), ALU.subtract).then_inc(s_x1l, 1)

            def weights_low(m, k):
                dve.wait_ge(s_wh[m], k + 1)
                nc.vector.tensor_tensor(wl[:, k, m, :], w_raw[:, k, m, :], wh[:, k, m, :].bitcast(f32),
                                        ALU.subtract).then_inc(s_wl[m], 1)

            def hidden_low(u):
                dve.wait_ge(s_hh, u + 1)
                r = UNITS[u][0]
                nc.vector.scalar_tensor_tensor(out=packed(hl[:, u % NBUF, :], r),
                                               in0=packed(h_ps[u % NBUF][:, :], r), scalar=0.0,
                                               in1=packed(hh[:, u % NBUF, :].bitcast(f32), r), op0=ALU.max,
                                               op1=ALU.subtract).then_inc(s_hl, 1)

            def slot_output(r):
                dve.wait_ge(s_mm2, (r + 1) * FC)
                dve.wait_ge(s_out, reads_until(r - 1))
                kind_of, k = RUNS[r]
                if kind_of == "extra":
                    nc.vector.tensor_copy(ex[:, k, :], acc_of(r)).then_inc(s_out, 1)
                    return
                dve.wait_ge(s_wslot, 1)
                p, i = divmod(k, 2)
                for j in range(2):
                    w, src, dst = wslot[:, 4 * p + 2 * i + j:4 * p + 2 * i + j + 1], acc_of(r)[:, j, :], es[:, 2 * p + j, :]
                    if i == 0:
                        ins = nc.vector.tensor_scalar(dst, src, w, None, ALU.mult)
                    else:
                        ins = nc.vector.scalar_tensor_tensor(out=dst, in0=src, scalar=w, in1=dst, op0=ALU.mult,
                                                             op1=ALU.add)
                    ins.then_inc(s_out, 1)

            def extra_output(p, x):
                if x == 0:
                    dve.wait_ge(s_out, reads_until(FIRST_SLOT + EXTRA + 2 * p + 1))
                else:
                    dve.wait_ge(s_es_base, p + 1)
                n, dst = 2 * B + x * PR + p, es[:, 2 * p + 1, :]
                ins = nc.vector.scalar_tensor_tensor(out=dst, in0=ex[:, x, :], scalar=wslot[:, n:n + 1],
                                                     in1=dst, op0=ALU.mult, op1=ALU.add)
                ins.then_inc(s_es_base if x < EXTRA - 1 else s_es, 1)

            def gate_products(h):
                dve.wait_ge(s_ga, h + 1)
                nc.vector.scalar_tensor_tensor(out=gprod[:, h, :, :],
                                               in0=gh_ps[:, 0:HB].unsqueeze(2).to_broadcast([P, HB, G]), scalar=0.0,
                                               in1=gw2[:, :].unsqueeze(1).to_broadcast([P, HB, G]), op0=ALU.max,
                                               op1=ALU.mult).then_inc(s_gp, 1)

            def gate_shift(h):
                dve.wait_ge(s_gl, h + 1)
                logits = gl_ps[:, 0:HB * G].rearrange("p (b g) -> p b g", g=G)
                link(nc.vector.tensor_reduce(gmax[:, h, :], logits, AX.X, ALU.max))
                nc.vector.tensor_tensor(ge[:, h, :, :], logits, gmax[:, h, :].unsqueeze(2).to_broadcast([P, HB, G]),
                                        ALU.subtract).then_inc(s_gd, 1)

            def gate_weights(h):
                dve.wait_ge(s_ge, h + 1)
                link(nc.vector.tensor_reduce(gsum[:, h, :], ge[:, h, :, :], AX.X, ALU.add))
                link(nc.vector.reciprocal(grec[:, h, :], gsum[:, h, :]))
                nc.vector.tensor_tensor(g[:, h, :, :], ge[:, h, :, :], grec[:, h, :].unsqueeze(2).to_broadcast([P, HB, G]),
                                        ALU.mult).then_inc(s_g, 1)
                dve.wait_ge(s_g, h + 1)

            done = {}

            def mixture_term(i, b):
                if b in done:
                    dve.wait_ge(s_dve, done[b])
                h, j = divmod(b, HB)
                ins = nc.vector.scalar_tensor_tensor(
                    out=comb[:, b, :], in0=mix[:, i, seq(b)] if h == 0 or i < G - 1 else last_acc[:, seq(j)],
                    scalar=g[:, h, j, i:i + 1], in1=comb[:, b, :] if i else x1T[:, seq(b)],
                    op0=ALU.mult, op1=ALU.add)
                if i == G - 1:
                    ins.then_inc(s_comb, 1)
                else:
                    chain[0] += 1
                    ins.then_inc(s_dve, 1)
                    done[b] = chain[0]

            dve.wait_ge(s_cols, 1)
            nc.vector.tensor_copy(cols_c[:, 0, :], b1_ps[:, 0:B]).then_inc(s_colsc, 1)
            dve.wait_ge(s_xt, 1)
            nc.vector.tensor_copy(xT[:, cols(0)], xt_ps[0][:, :]).then_inc(s_xtc, 1)
            sort_by_type()
            slot_tables()
            dve.wait_ge(s_cols, 2)
            nc.vector.tensor_copy(cols_c[:, 1:3, :].rearrange("p n b -> p (n b)"),
                                  cols_ps[:, 0:2 * B]).then_inc(s_colsc, 1)
            extra_tables()
            norm_stats(0)
            norm_stats(1)
            extra_tables_ends()
            dve.wait_ge(s_colsc, 2)
            norm_apply(0)
            norm_apply(1)
            x1_transposed(0)
            x1_transposed(1)
            x1_low(0)
            x1_low(1)
            adapter_relu(1, (2, 3))
            for u, (r, c) in enumerate(UNITS):
                hidden_low(u)
                if u == 0:
                    weights_low(1, 0)
                if u in (0, 1):
                    norm_stats(u + 2)
                if u in (2, 3):
                    norm_apply(u)
                if u in (4, 5):
                    x1_transposed(u - 2)
                if u == 6:
                    x1_low(2)
                    x1_low(3)
                if u == 8:
                    dve.wait_ge(s_gv, 16)
                    link(nc.vector.tensor_scalar(gv[:, :, :], gv[:, :, :], 10.0, None, ALU.mult))
                    link(nc.vector.tensor_reduce(gm[:, :], gv[:, :, :], AX.X, ALU.max))
                    nc.vector.tensor_tensor(gq[:, :, :], gv[:, :, :], gm[:, :].unsqueeze(2).to_broadcast([P, T, E]),
                                            ALU.subtract).then_inc(s_gvq, 1)
                if u == 10:
                    dve.wait_ge(s_gve, 1)
                    link(nc.vector.tensor_reduce(gs[:, :], gq[:, :, :], AX.X, ALU.add))
                    link(nc.vector.reciprocal(gm[:, :], gs[:, :]))
                    nc.vector.tensor_tensor(gq[:, :, :], gq[:, :, :], gm[:, :].unsqueeze(2).to_broadcast([P, T, E]),
                                            ALU.mult).then_inc(s_gvp, 1)
                if u == 11:
                    slot_weights()
                if u == 13:
                    slot_weights_ends()
                if r and RUNS[r - 1][0] != "shared" and c == 1:
                    slot_output(r - 1)
                if r and RUNS[r - 1][0] == "base" and RUNS[r - 1][1] % 2 and c > 1:
                    for x in (c - 2,) if r < END_SLOT else range(EXTRA) if c == 2 else ():
                        extra_output(RUNS[r - 1][1] // 2, x)
                for h in range(NH):
                    if u == GATES[h] + 2:
                        gate_products(h)
                        gate_shift(h)
                    if u == GATES[h] + 3:
                        gate_weights(h)
                    for at, i, b in MIXTURE_AT[h]:
                        if u == GATES[h] + at:
                            if h and i and b == HB:
                                dve.wait_ge(s_out, reads_until(LAST - 3 + i))
                            mixture_term(i, b)
            dve.wait_ge(s_mm2, len(UNITS))
            for b in range(HB, B):
                if b == B - PAIR:
                    dve.wait_ge(s_part, len(BY_POOL) + 1)
                mixture_term(G - 1, b)
            dve.wait_ge(s_ot, PAIRS)
            dve.wait_ge(s_o, PAIRS - 1)
            nc.vector.tensor_copy(o_sb[:, B - PAIR:B, :].rearrange("p b d -> p (b d)"),
                                  t_ps[PAIRS - 1][:, 0:PAIR * S]).then_inc(s_o, 1)

        @block.tensor
        def _(pe):
            def transpose_x(h):
                pe.wait_ge(s_x[h], 16)
                for j in range(HB):
                    mm = nc.tensor.transpose(xt_ps[h][:, seq(j)], x_in[:, h * HB + j, :], ident[:, :])
                mm.then_inc(s_xt, 1)

            def adapter_in(h):
                pe.wait_ge(s_xtc, h + 1)
                pe.wait_ge(s_w1[h], 16 * HB)
                if h:
                    pe.wait_ge(s_h0a[h - 1], HB)
                nc.tensor.matmul(w1_ps[:, :], W1s[:, half(h), :], xT[:, cols(h)],
                                 start=True, stop=True).then_inc(s_h0, 1)

            def residual(h):
                if h:
                    pe.wait_ge(s_xtc, 1)
                nc.tensor.matmul(y_ps[h][:, :], ident[:, :], x_in[:, half(h), :], start=True, stop=False,
                                 skip_group_check=True)

            def residual_bias(h):
                for j in range(HB):
                    nc.tensor.matmul(y_ps[h][:, seq(j)], onehot[:, h * HB + j:h * HB + j + 1].to_broadcast([L, P]),
                                     par_l[:, 0, :], start=False, stop=False, skip_group_check=True)

            def adapter_out(h):
                pe.wait_ge(s_w2[h], 16 * HB)
                pe.wait_ge(s_h0a[h], HB)
                for j in range(HB):
                    mm = nc.tensor.matmul(y_ps[h][:, seq(j)], hbd[:, h, seq(j)], W2s[:, h, :],
                                          start=False, stop=(j == HB - 1), skip_group_check=True)
                mm.then_inc(s_y, 1)

            def transpose_z(n):
                h, k = divmod(n, 2)
                pe.wait_ge(s_z, PAIR * (n + 1))
                if n == 2:
                    pe.wait_ge(s_h0a[1], HB)
                for i in range(PAIR):
                    mm = nc.tensor.transpose(zt_ps[h][k][:, seq(i)], z[:, n * PAIR + i, :], ident[:, :])
                mm.then_inc(s_zt, 1)

            def first_product(u):
                r, c = UNITS[u]
                run, w = RUNS[r], set_of(r)
                if c == 0 and r < END_SLOT:
                    pe.wait_ge(s_wh[w], 1)
                    pe.wait_ge(s_wl[w], 1)
                if u == 0:
                    pe.wait_ge(s_x1h, PAIRS // 2)
                if c == 0 and run == ("extra", 0):
                    pe.wait_ge(s_xe, 16 * EXTRA)
                if c == 0 and run[0] == "base" and run[1] % 2 == 0:
                    pe.wait_ge(s_xs[run[1] // 2], 32)
                if u >= NBUF:
                    pe.wait_ge(s_hl, u - NBUF + 1)
                dst, chunk = packed(h_ps[u % NBUF][:, :], r), slice(c * P, (c + 1) * P)
                nc.tensor.matmul(dst, wh[:, 0, buf(w), chunk], x_of(r, 0), start=True, stop=False)
                nc.tensor.matmul(dst, wl[:, 0, buf(w), chunk], x_of(r, 0), start=False, stop=False)
                if u == 0:
                    pe.wait_ge(s_x1l, PAIRS // 2)
                nc.tensor.matmul(dst, wh[:, 0, buf(w), chunk], x_of(r, 1), start=False, stop=True).then_inc(s_mm1, 1)

            def second_product(u):
                r, c = UNITS[u]
                w, dst, chunk = set_of(r), acc_of(r), slice(c * P, (c + 1) * P)
                hi, lo = (packed(v[:, u % NBUF, :], r) for v in (hh, hl))
                if c == 0 and r < END_SLOT:
                    pe.wait_ge(s_wh[w], 2)
                    pe.wait_ge(s_wl[w], 2)
                pe.wait_ge(s_hh, u + 1)
                if c == 0 and r >= 2:
                    pe.wait_ge(s_out, reads_until(r - 2))
                nc.tensor.matmul(dst, wh[:, 1, buf(w), chunk], hi, start=(c == 0), stop=False)
                nc.tensor.matmul(dst, wl[:, 1, buf(w), chunk], hi, start=False, stop=False)
                pe.wait_ge(s_hl, u + 1)
                nc.tensor.matmul(dst, wh[:, 1, buf(w), chunk], lo, start=False, stop=(c == FC - 1)).then_inc(s_mm2, 1)

            def gate_hidden(h):
                for i in range(G):
                    mm = nc.tensor.matmul(gh_ps[:, 0:HB], gw1[:, i, :], mix[:, i, cols(h)][:, 0:HT:S],
                                          start=(i == 0), stop=(i == G - 1))
                mm.then_inc(s_ga, 1)

            def gate_logits(h):
                pe.wait_ge(s_gp, h + 1)
                nc.tensor.matmul(gl_ps[:, 0:HB * G], ones[:, :], gprod[:, h, :, :].rearrange("p b g -> p (b g)"),
                                 start=True, stop=True).then_inc(s_gl, 1)

            def transpose_result(n):
                if n < PAIRS // 2 and results.index(n):
                    pe.wait_ge(s_o, results.index(n))
                for i in range(PAIR):
                    b, dst = n * PAIR + i, t_ps[n][:, seq(i)]
                    if b in BY_POOL:
                        pe.wait_ge(s_part, BY_POOL.index(b) + 1)
                    else:
                        pe.wait_ge(s_comb, b + 1 - len(BY_POOL))
                    mm = nc.tensor.transpose(dst, comb[:, b, :], ident[:, :])
                mm.then_inc(s_ot, 1)

            def raise_clock():
                for _ in range(WARM):
                    nc.tensor.matmul(acc[1][:, :], warm[:, 0:P], warm[:, :], start=True, stop=True)

            pe.wait_ge(s_warm, 1)
            raise_clock()
            pe.wait_ge(s_ident, 1)
            pe.wait_ge(s_onehot, 1)
            pe.wait_ge(s_b1in, 16)
            nc.tensor.matmul(b1_ps[:, 0:B], b1_l[:, :, :].rearrange("l r a -> l (r a)"), onehot[:, :],
                             start=True, stop=True).then_inc(s_cols, 1)
            transpose_x(0)
            residual(0)
            adapter_in(0)
            pe.wait_ge(s_par, 16)
            residual_bias(0)
            pe.wait_ge(s_gb, 32)
            for n in (1, 2):
                mm = nc.tensor.matmul(cols_ps[:, (n - 1) * B:n * B], par_l[:, n, :], onehot[:, :],
                                      start=True, stop=True)
            mm.then_inc(s_cols, 1)
            adapter_out(0)
            transpose_x(1)
            residual(1)
            residual_bias(1)
            transpose_z(0)
            transpose_z(1)
            adapter_in(1)
            for u in range(AHEAD):
                first_product(u)
            adapter_out(1)
            for u, (r, c) in enumerate(UNITS):
                if u + AHEAD < len(UNITS):
                    first_product(u + AHEAD)
                for h in range(NH):
                    if u == GATES[h] + 1:
                        gate_logits(h)
                second_product(u)
                if u == 3:
                    transpose_z(2)
                    transpose_z(3)
                for h in range(NH):
                    if u == GATES[h]:
                        pe.wait_ge(s_out, reads_until((END_SLOT - 1, GATE_RUN)[h]))
                        if h == 0:
                            pe.wait_ge(s_gate, 32)
                            pe.wait_ge(s_ones, 1)
                            pe.wait_ge(s_ret, 16 * B)
                        gate_hidden(h)
                if u - GATES[0] in RESULTS:
                    transpose_result(RESULTS[u - GATES[0]])
            for n in range(PAIRS // 2, PAIRS):
                transpose_result(n)


_INS = ['x', 'itok_B_0_8', 'itok_B_0_2', 'L0_cond_W1', 'L0_cond_b1', 'L0_cond_W2', 'L0_cond_b2', 'L0_cond_gamma',
        'L0_cond_beta', 'L1_cond_expert_wi', 'L1_cond_expert_wo', 'L1_cond_share_wi', 'L1_cond_share_wo',
        'L1_cond_gate_vecs', 'L1_cond_gate_w1', 'L1_cond_gate_w2']


def kernel(**inputs):
    import numpy as _np
    import concourse.bacc as _bacc
    from concourse import mybir as _mybir
    from concourse.bass_utils import run_bass_kernel_spmd as _run

    nc = _bacc.Bacc("TRN2", target_bir_lowering=False, num_devices=1)
    arrays, args = {}, []
    for name in _INS:
        a = _np.ascontiguousarray(inputs[name])
        arrays[f"in_{name}_dram"] = a
        args.append(nc.dram_tensor(f"in_{name}_dram", a.shape, _mybir.dt.from_np(a.dtype), kind="ExternalInput").ap())
    shape = inputs['x'].shape
    args.append(nc.dram_tensor("out_0_dram", shape, _mybir.dt.from_np(_np.dtype('float32')),
                               kind="ExternalOutput").ap())
    conditional_residual_mlps(nc, *args)
    r = _run(nc, [arrays], core_ids=[0])
    return r.results[0]["out_0_dram"]
```
